# Optimizing a Trainium2 kernel written in Bass

```python
import numpy as np
import jax
import jax.numpy as jnp

def _softmax(x, axis=-1):
    return jax.nn.softmax(x, axis=axis)

def _gelu(x):
    return jax.nn.gelu(x, approximate=True)

def _silu(x):
    return jax.nn.silu(x)

def _sigmoid(x):
    return jax.nn.sigmoid(x)

def _layernorm(x, axis=-1, eps=1e-05):
    m = jnp.mean(x, axis=axis, keepdims=True)
    v = jnp.var(x, axis=axis, keepdims=True)
    return (x - m) / jnp.sqrt(v + eps)

def _scatter_add(tgt, idx, src, axis=0):
    return tgt.at[idx].add(src)

def _segment_sum(src, seg, n):
    return jax.ops.segment_sum(src, seg, n)
kernel_name = 'mk_gnn_resnorm_d2_gnn_r32_e9491b'

def setup_inputs(seed: int=0):
    np.random.seed(seed)
    _w = jnp.asarray

    def _rec_inputs():
        import jax
        import jax.numpy as jnp
        _gk = jax.random.key(seed)
        x = -0.000202 + 1 * jax.random.normal(jax.random.fold_in(_gk, 1), (3125, 128), jnp.float32)
        _s = jax.random.randint(jax.random.fold_in(_gk, 2), (25000,), 0, 3125, jnp.int32)
        _d = jax.random.randint(jax.random.fold_in(_gk, 3), (25000,), 0, 3125, jnp.int32)
        _loop = jnp.arange(3125, dtype=jnp.int32)
        src = jnp.concatenate([_s, _d, _loop])
        dst = jnp.concatenate([_d, _s, _loop])
        _o = jnp.argsort(dst, stable=True)
        src = src[_o]
        dst = dst[_o]
        edge_attr_128 = -8.513e-05 + 0.999844 * jax.random.normal(jax.random.fold_in(_gk, 12), (53125, 128), jnp.float32)
        edge_type_32 = jax.random.randint(jax.random.fold_in(_gk, 13), (53125,), 0, 32, jnp.int32)
        edge_weight1 = jax.random.uniform(jax.random.fold_in(_gk, 14), (53125, 1), jnp.float32, 0.0, 0.999998)
        return (x, src, dst, edge_attr_128, edge_type_32, edge_weight1)
    x, src, dst, edge_attr_128, edge_type_32, edge_weight1 = _rec_inputs()

    def _L0_gnn_setup():
        import jax, jax.numpy as jnp
        import numpy as np
        N_NODES = 50000
        N_EDGES = 15625
        IN_FEAT = 128
        OUT_FEAT = 128
        NUM_RELS = 32
        NUM_BASES = 8
        key = jax.random.key(seed)
        ks = jax.random.split(key, 8)
        h = jax.random.normal(ks[0], (N_NODES, IN_FEAT), dtype=jnp.float32)
        src = jax.random.randint(ks[1], (N_EDGES,), 0, N_NODES, dtype=jnp.int32)
        dst = jax.random.randint(ks[2], (N_EDGES,), 0, N_NODES, dtype=jnp.int32)
        etype = jax.random.randint(ks[3], (N_EDGES,), 0, NUM_RELS, dtype=jnp.int32)
        norm = jax.random.uniform(ks[4], (N_EDGES, 1), dtype=jnp.float32)
        weight = jax.random.normal(ks[5], (NUM_BASES, IN_FEAT, OUT_FEAT), dtype=jnp.float32) * 0.05
        w_comp = jax.random.normal(ks[6], (NUM_RELS, NUM_BASES), dtype=jnp.float32) * 0.3
        bias_param = jax.random.normal(ks[7], (OUT_FEAT,), dtype=jnp.float32) * 0.05
        return {'h': h, 'src': src, 'dst': dst, 'etype': etype, 'norm': norm, 'weight': weight, 'w_comp': w_comp, 'bias_param': bias_param}
    _L0_gnn_all = _L0_gnn_setup()
    _L0_gnn_in = {k: v for k, v in _L0_gnn_all.items() if k in ('weight', 'w_comp', 'bias_param')}
    del _L0_gnn_all

    def _L1_gnn_setup():
        import jax, jax.numpy as jnp
        import numpy as np
        N_NODES = 50000
        N_EDGES = 20000
        EMB = 128
        BN_EPS = 1e-05
        key = jax.random.key(seed)
        ks = jax.random.split(key, 8)
        node_feat = jax.random.normal(ks[0], (N_NODES, EMB), dtype=jnp.float32)
        edge_feat = jax.random.normal(ks[1], (N_EDGES, EMB), dtype=jnp.float32)
        src = jax.random.randint(ks[2], (N_EDGES,), 0, N_NODES, dtype=jnp.int64)
        dst = jax.random.randint(ks[3], (N_EDGES,), 0, N_NODES, dtype=jnp.int64)
        eps = jnp.zeros((1,), dtype=jnp.float32)
        W1 = jax.random.normal(ks[4], (EMB, 2 * EMB), dtype=jnp.float32) * (1.0 / np.sqrt(EMB))
        b1 = jnp.zeros((2 * EMB,), dtype=jnp.float32)
        gamma = jnp.ones((2 * EMB,), dtype=jnp.float32)
        beta = jnp.zeros((2 * EMB,), dtype=jnp.float32)
        W2 = jax.random.normal(ks[5], (2 * EMB, EMB), dtype=jnp.float32) * (1.0 / np.sqrt(2 * EMB))
        b2 = jnp.zeros((EMB,), dtype=jnp.float32)
        return {'node_feat': node_feat, 'edge_feat': edge_feat, 'src': src, 'dst': dst, 'eps': eps, 'W1': W1, 'b1': b1, 'gamma': gamma, 'beta': beta, 'W2': W2, 'b2': b2}
    _L1_gnn_all = _L1_gnn_setup()
    _L1_gnn_in = {k: v for k, v in _L1_gnn_all.items() if k in ('eps', 'W1', 'b1', 'gamma', 'beta', 'W2', 'b2')}
    del _L1_gnn_all
    return {'x': x, 'src': src, 'dst': dst, 'edge_attr_128': edge_attr_128, 'edge_type_32': edge_type_32, 'edge_weight1': edge_weight1, 'L0_gnn_weight': _L0_gnn_in['weight'], 'L0_gnn_w_comp': _L0_gnn_in['w_comp'], 'L0_gnn_bias_param': _L0_gnn_in['bias_param'], 'L1_gnn_eps': _L1_gnn_in['eps'], 'L1_gnn_W1': _L1_gnn_in['W1'], 'L1_gnn_b1': _L1_gnn_in['b1'], 'L1_gnn_gamma': _L1_gnn_in['gamma'], 'L1_gnn_beta': _L1_gnn_in['beta'], 'L1_gnn_W2': _L1_gnn_in['W2'], 'L1_gnn_b2': _L1_gnn_in['b2']}

def reference(x, src, dst, edge_attr_128, edge_type_32, edge_weight1, L0_gnn_weight, L0_gnn_w_comp, L0_gnn_bias_param, L1_gnn_eps, L1_gnn_W1, L1_gnn_b1, L1_gnn_gamma, L1_gnn_beta, L1_gnn_W2, L1_gnn_b2):
    import jax
    import jax.numpy as jnp

    def _L0_gnn_ref(h, src, dst, etype, norm, weight, w_comp, bias_param):
        import jax, jax.numpy as jnp
        import numpy as np
        N_NODES = 50000
        N_EDGES = 15625
        IN_FEAT = 128
        OUT_FEAT = 128
        NUM_RELS = 32
        NUM_BASES = 8
        hsrc = h[src]
        coef = w_comp[etype]
        msg = jnp.zeros((hsrc.shape[0], weight.shape[2]), dtype=h.dtype)
        for b in range(weight.shape[0]):
            msg = msg + hsrc @ weight[b] * coef[:, b][:, None]
        msg = msg * norm
        node_repr = jax.ops.segment_sum(msg, dst, num_segments=h.shape[0])
        node_repr = node_repr + bias_param
        return jax.nn.relu(node_repr)

    def _L1_gnn_ref(node_feat, edge_feat, src, dst, eps, W1, b1, gamma, beta, W2, b2):
        import jax, jax.numpy as jnp
        import numpy as np
        N_NODES = 50000
        N_EDGES = 20000
        EMB = 128
        BN_EPS = 1e-05
        msg = node_feat[src] + edge_feat
        neigh = jax.ops.segment_sum(msg, dst, num_segments=node_feat.shape[0])
        rst = (1.0 + eps[0]) * node_feat + neigh
        h = rst @ W1 + b1
        mean = jnp.mean(h, axis=0)
        var = jnp.var(h, axis=0)
        h = (h - mean) * jax.lax.rsqrt(var + BN_EPS) * gamma + beta
        h = jax.nn.relu(h)
        out = h @ W2 + b2
        return out
    x = _layernorm(x + _L0_gnn_ref(x, src, dst, edge_type_32, edge_weight1, L0_gnn_weight, L0_gnn_w_comp, L0_gnn_bias_param), axis=-1)
    x = _layernorm(x + _L1_gnn_ref(x, edge_attr_128, src, dst, L1_gnn_eps, L1_gnn_W1, L1_gnn_b1, L1_gnn_gamma, L1_gnn_beta, L1_gnn_W2, L1_gnn_b2), axis=-1)
    return x

_drawn_inputs = setup_inputs


def setup_inputs(seed=0):
    import zlib

    import numpy as np

    out = dict(_drawn_inputs(seed))
    spreads = {'L1_gnn_b1': (0.0, 0.1),
     'L1_gnn_gamma': (1.0, 0.2),
     'L1_gnn_beta': (0.0, 0.1),
     'L1_gnn_b2': (0.0, 0.1)}
    factors = {}
    for name, (base, spread) in spreads.items():
        noise = np.random.default_rng([zlib.crc32(name.encode()), seed]).standard_normal(out[name].shape)
        drawn = base * np.exp(spread * noise) if base else spread * noise
        out[name] = jnp.asarray(drawn.astype(out[name].dtype))
    for name, factor in factors.items():
        out[name] = (out[name] * factor).astype(out[name].dtype)
    return out
```

```python
from contextlib import ExitStack

import concourse.bass as bass
from concourse import mybir

F32 = mybir.dt.float32
I32 = mybir.dt.int32
ALU = mybir.AluOpType
ACT = mybir.ActivationFunctionType
AX_X = mybir.AxisListType.X
ENGINE = mybir.EngineType

P = 128
WIN = 16
GROUP = 8
RING = 4
CHUNK = 512
LN_EPS = 1e-5
BN_EPS = 1e-5


def gnn_resnorm_kernel(nc, x, src, dst, edge_attr, etype, norm, weight, w_comp, bias0,
                       eps, w1, b1, gamma, beta, w2, b2, out):
    N, F = x.shape
    E = src.shape[0]
    B = weight.shape[0]
    R = w_comp.shape[0]
    H = w1.shape[1]
    assert F == P and H == 2 * P and R == 32

    T = -(-E // P)
    FRESH = E - (T - 1) * P
    TQ = T // 4
    assert T == 4 * TQ and T % (GROUP * RING) == 0 and 0 < FRESH <= P
    GROUPS = T // GROUP
    NP = N + WIN - 1
    WIDE = 125
    WIDES = -(-N // WIDE)
    assert WIDES * WIDE <= NP and 4 * WIDE <= 512
    CHUNKS = N // CHUNK
    REST = N - CHUNKS * CHUNK
    CT = CHUNK // P
    assert CHUNKS % 2 == 0 and 0 < REST <= P
    PQ = 13
    PIECES = TQ // PQ
    assert TQ % PQ == 0 and PIECES % 2 == 0 and PQ * 4 * B <= 512 and PQ >= GROUP

    x1_table = nc.dram_tensor("x1_table", (N, F), F32, kind="Internal").ap()

    with ExitStack() as ctx:
        def sb(name, shape, dt=F32):
            return ctx.enter_context(nc.sbuf_tensor(name, shape, dt))

        def sem(name):
            return ctx.enter_context(nc.semaphore(name))

        attrs = sb("attrs", [P, RING * GROUP, F])
        src_rows, dst_rows = (attrs[0:TQ, 4 * i:4 * i + 4, :].bitcast(I32) for i in range(2))
        norm_rows, srcf_rows, dstf_rows, rel_rows = (attrs[0:TQ, 4 * i:4 * i + 4, :] for i in range(2, 6))
        base_col = sb("base_col", [TQ, 4])
        high_col = sb("high_col", [TQ, 4])
        span_col = sb("span_col", [TQ, 4])
        src_t = sb("src_t", [P, T])
        dst_t = sb("dst_t", [P, T])
        rel_t = sb("rel_t", [P, T])
        norm_t = sb("norm_t", [P, T])
        base_row = sb("base_row", [1, T], I32)
        span_max = sb("span_max", [1, 1])
        wide_flag = sb("wide_flag", [1, 1], I32)
        coef = sb("coef", [P, T, B])
        etype_bc = sb("etype_bc", [P, 2, PQ * P], I32)
        etype_hot = sb("etype_hot", [P, 2, PQ * P])
        relation_col = sb("relation_col", [P, 1])
        comp_diag = sb("comp_diag", [P, 4, B])
        ident = sb("ident", [P, P])
        iota_win = sb("iota_win", [P, WIN])
        iota_wide = sb("iota_wide", [P, WIDE])
        wide_starts = sb("wide_starts", [P, WIDES])
        iota_col = sb("iota_col", [P, 1])
        own_col = sb("own_col", [P, 1])
        zero_col = sb("zero_col", [P, 1])
        ln_eps_col = sb("ln_eps_col", [P, 1])
        w_base = sb("w_base", [P, B, F])
        w1_sb = sb("w1_sb", [P, H])
        w2_sb = sb("w2_sb", [P, 2, F])
        bias0_col = sb("bias0_col", [P, 1])
        b1_col = sb("b1_col", [P, 2])
        gamma_col = sb("gamma_col", [P, 2])
        beta_col = sb("beta_col", [P, 2])
        b2_col = sb("b2_col", [P, 1])
        eps_col = sb("eps_col", [P, 1])
        one_eps = sb("one_eps", [P, 1])
        sums = sb("sums", [P, B + 1, NP])
        x1_t = etype_hot[:, :, :].rearrange("p s e -> p (s e)")[:, 0:N]
        gathered = sb("gathered", [P, RING * GROUP, F])
        src_slots = sb("src_slots", [P, RING * GROUP], I32)
        hot = sb("hot", [P, 2, GROUP, WIN])
        weighted = sb("weighted", [P, 2, GROUP, B, WIN])
        wide_hot_sb = sb("wide_hot_sb", [P, WIDE])
        wide_weighted = weighted[:, :, :, :, :].rearrange("p s t b n -> p (s t b n)")[:, 0:B * WIDE] \
            .rearrange("p (b n) -> p b n", n=WIDE)
        node_stage = attrs[:, 0:2 * CT, :].rearrange("p (s t) f -> p s t f", s=2)
        layer_stage = attrs[:, 2 * CT:4 * CT, :].rearrange("p (s t) f -> p s (t f)", s=2)
        out_stage = gathered
        hidden = sums[:, 0:2, 0:N]
        relu_stage = sums[:, 2:4, 0:2 * CHUNK].rearrange("p s (j n) -> p s j n", j=2)
        bn_part = sb("bn_part", [P, 2, CHUNKS + 1, 6])
        bn_mv = sb("bn_mv", [P, 2, 2])
        bn_std = sb("bn_std", [P, 2])
        bn_rstd = sb("bn_rstd", [P, 2])
        bn_scale = sb("bn_scale", [P, 2])
        bn_ms = sb("bn_ms", [P, 2])
        bn_shift = sb("bn_shift", [P, 2])
        ln_part = sb("ln_part", [P, 2, CT, 6])
        ln_mv = sb("ln_mv", [P, 2, CT, 2])
        ln_std = sb("ln_std", [P, 2, CT])
        ln_rstd = sb("ln_rstd", [P, 2, CT])

        psum = ctx.enter_context(nc.psum_tensor("psum", [P, 8, 512], F32))

        def tile_psum(slot, i):
            c = (i % 3) * (B + 1) * WIN
            return psum[:, 3 * slot + i // 3, c:c + (B + 1) * WIN].rearrange("p (b n) -> p b n", n=WIN)

        def wide_psum(b):
            return psum[:, b // 4, (b % 4) * WIDE:(b % 4 + 1) * WIDE]

        const_ready = sem("const_ready")
        src_in = sem("src_in")
        rows_in = sem("rows_in")
        comp_zeroed = sem("comp_zeroed")
        comp_in = sem("comp_in")
        weights_in = sem("weights_in")
        prep = sem("prep")
        srcf_ready = sem("srcf_ready")
        rows_ready = sem("rows_ready")
        src_turned = sem("src_turned")
        turned = sem("turned")
        src_t_ready = sem("src_t_ready")
        flag_ready = sem("flag_ready")
        etype_in = [sem(f"etype_in{i}") for i in range(2)]
        hot_built = sem("hot_built")
        coef_mm = sem("coef_mm")
        coef_ready = sem("coef_ready")
        zeroed = sem("zeroed")
        slots_ready = [sem(f"slots_ready{r}") for r in range(2)]
        gather_in = [[sem(f"gather_in{r}_{i}") for i in range(RING)] for r in range(2)]
        attrs_in = [sem(f"attrs_in{i}") for i in range(RING)]
        hot_ready = [sem(f"hot_ready{r}") for r in range(2)]
        select_ready = sem("select_ready")
        group_mm = [sem(f"group_mm{r}") for r in range(2)]
        added = [sem(f"added{r}") for r in range(2)]
        round_done = [sem(f"round_done{r}") for r in range(2)]
        wide_slot = [sem(f"wide_slot{r}") for r in range(2)]
        wide_gather = [sem(f"wide_gather{r}") for r in range(2)]
        wide_attr = sem("wide_attr")
        wide_hot = [sem(f"wide_hot{r}") for r in range(2)]
        wide_select = sem("wide_select")
        wide_mm = [sem(f"wide_mm{r}") for r in range(2)]
        wide_add = [sem(f"wide_add{r}") for r in range(2)]
        wide_tile = [sem(f"wide_tile{r}") for r in range(2)]
        x_in = [sem(f"x_in{i}") for i in range(2)]
        agg_mm = sem("agg_mm")
        agg_relu = sem("agg_relu")
        agg_turned = sem("agg_turned")
        res_ready = [sem(f"res_ready{r}") for r in range(2)]
        ln_stats = [sem(f"ln_stats{r}") for r in range(2)]
        ln_var = [sem(f"ln_var{r}") for r in range(2)]
        ln_std_ready = [sem(f"ln_std_ready{r}") for r in range(2)]
        ln_rstd_ready = [sem(f"ln_rstd_ready{r}") for r in range(2)]
        x1_ready = sem("x1_ready")
        x1_out = [sem(f"x1_out{i}") for i in range(2)]
        x1_turned = sem("x1_turned")
        x1_t_ready = sem("x1_t_ready")
        rst_ready = sem("rst_ready")
        hidden_mm = sem("hidden_mm")
        hidden_ready = sem("hidden_ready")
        bn_step = sem("bn_step")
        bn_var = sem("bn_var")
        bn_std_ready = sem("bn_std_ready")
        bn_ready = sem("bn_ready")
        relu_ready = sem("relu_ready")
        out_mm = sem("out_mm")
        out_t_ready = sem("out_t_ready")
        out_turned = sem("out_turned")
        out_ready = sem("out_ready")
        out_done = sem("out_done")

        passed = sem("passed")

        block = ctx.enter_context(nc.Block())

        def wait_alone(engine, semaphore, value):
            engine.wait_ge(semaphore, value)
            engine.sem_inc(passed, 1)

        def read_flag(engine, which):
            engine.wait_ge(flag_ready, 1)
            return nc.values_load(wide_flag[0:1, 0:1], engines=(which,), min_val=0, max_val=1,
                                  skip_runtime_bounds_check_because="a comparison's result")

        def chunk_pipeline(engine, *stages):
            def step(k, s):
                for lag, stage in enumerate(stages):
                    if isinstance(k, int) and not 0 <= k - lag <= CHUNKS:
                        continue
                    rest = isinstance(k, int) and k - lag == CHUNKS
                    stage(k - lag, (s - lag) % 2, REST if rest else CHUNK)
            assert len(stages) <= 3
            step(0, 0)
            step(1, 1)
            with engine.Fori(1, CHUNKS // 2) as i:
                for s in range(2):
                    step(i * 2 + s, s)
            for k in range(CHUNKS, CHUNKS + len(stages)):
                step(k, k % 2)

        def tiles_of(n):
            return [(i, min(P, n - i * P)) for i in range(-(-n // P))]

        def span(k, n):
            return bass.ds(k * CHUNK, n)

        attr_tiles = edge_attr[0:(T - 1) * P, :].rearrange("(t p) f -> p t f", p=P)
        last_edges = slice(E - P, E)

        @block.sync
        def _(sp):
            def load_rows(rows, ap, signal):
                for q in range(4):
                    full = TQ if q < 3 else TQ - 1
                    lo = q * TQ * P
                    sp.dma_start(rows[0:full, q, :],
                                 ap[lo:lo + full * P].rearrange("(t e) -> t e", e=P)).then_inc(signal, 16)
                sp.dma_start(rows[TQ - 1:TQ, 3, :],
                             ap[last_edges].rearrange("(t e) -> t e", e=P)).then_inc(signal, 16)

            load_rows(src_rows, src, src_in)
            load_rows(dst_rows, dst, rows_in)
            load_rows(norm_rows, norm, rows_in)

            def load_relations(m, s, last):
                wait_alone(sp, hot_built, m + 1)
                for q in range(4):
                    most = (PQ - 1) * P
                    sp.dma_start(etype_bc[32 * q:32 * q + 32, s, 0:most],
                                 etype[bass.ds((m * PQ + q * TQ) * P, most)].partition_broadcast(32)
                                 ).then_inc(etype_in[s], 16)
                    one = etype[last_edges] if last and q == 3 else \
                        etype[bass.ds((m * PQ + q * TQ) * P + most, P)]
                    sp.dma_start(etype_bc[32 * q:32 * q + 32, s, most:PQ * P],
                                 one.partition_broadcast(32)).then_inc(etype_in[s], 16)

            with sp.Fori(0, PIECES // 2 - 1) as i:
                for s in range(2):
                    load_relations(i * 2 + s, s, False)
            for s in range(2):
                load_relations(PIECES - 2 + s, s, s == 1)

            wide = read_flag(sp, ENGINE.SP)
            with sp.If(wide < 1):
                def load_attrs(g, s, last):
                    wait_alone(sp, group_mm[0], g + 1)
                    lo = s * GROUP
                    sp.dma_start(attrs[:, lo:lo + GROUP - 1, :],
                                 attr_tiles[:, bass.ds(g * GROUP, GROUP - 1), :]).then_inc(attrs_in[s], 16)
                    sp.dma_start(attrs[:, lo + GROUP - 1, :],
                                 edge_attr[last_edges, :] if last else
                                 edge_attr[bass.ds((g * GROUP + GROUP - 1) * P, P), :]).then_inc(attrs_in[s], 16)

                with sp.Fori(0, GROUPS // RING - 1) as i:
                    for s in range(RING):
                        load_attrs(i * RING + s, s, False)
                for s in range(RING):
                    load_attrs(GROUPS - RING + s, s, s == RING - 1)
            with sp.Else():
                def load_attr(t, rows):
                    wait_alone(sp, wide_tile[0], t + 1)
                    sp.dma_start(attrs[:, 0, :], rows).then_inc(wide_attr, 16)

                with sp.Fori(0, T - 1) as t:
                    load_attr(t, edge_attr[bass.ds(t * P, P), :])
                load_attr(T - 1, edge_attr[last_edges, :])

            sp.wait_ge(round_done[0], 1)

            def rows_of(table, k, n):
                if n == CHUNK:
                    return table[bass.ds(k * CHUNK, CHUNK), :].rearrange("(t p) f -> p t f", p=P)
                return table[k * CHUNK:k * CHUNK + n, :]

            def stage_rows(s, n):
                return node_stage[:, s, :, :] if n == CHUNK else node_stage[0:n, s, 0, :]

            def load_x(k, s, n):
                sp.dma_start(stage_rows(s, n), rows_of(x, k, n)).then_inc(x_in[s], 16)

            def store_x1(i, k, s, n):
                wait_alone(sp, x1_ready, (k + 2) * CT + len(tiles_of(n)))
                sp.dma_start(rows_of(x1_table, k, n), stage_rows(s, n)).then_inc(x1_out[s], 16)

            def reload(i, k, s, n):
                wait_alone(sp, x1_out[s], i * 16 + 16)
                wait_alone(sp, x1_turned, k - 1)
                load_x(k, s, n)

            load_x(0, 0, CHUNK)
            load_x(1, 1, CHUNK)
            with sp.Fori(0, CHUNKS // 2 - 1) as i:
                for s in range(2):
                    store_x1(i, i * 2 + s, s, CHUNK)
                    reload(i, i * 2 + s + 2, s, CHUNK)
            store_x1(CHUNKS // 2 - 1, CHUNKS - 2, 0, CHUNK)
            reload(CHUNKS // 2 - 1, CHUNKS, 0, REST)
            store_x1(CHUNKS // 2 - 1, CHUNKS - 1, 1, CHUNK)
            store_x1(CHUNKS // 2, CHUNKS, 0, REST)
            sp.wait_ge(x1_out[0], 16 * (CHUNKS // 2 + 1))
            sp.wait_ge(x1_out[1], 16 * (CHUNKS // 2))

            def store_out(k, s, n):
                wait_alone(sp, out_ready, (k + 2) * CT + len(tiles_of(n)))
                sp.dma_start(rows_of(out, k, n), out_stage[:, bass.ds(k * CT, CT), :] if n == CHUNK
                             else out_stage[0:n, k * CT, :]).then_inc(out_done, 16)

            chunk_pipeline(sp, store_out)
            sp.wait_ge(out_done, 16 * (CHUNKS + 1))

        @block.gpsimd
        def _(pool):
            nc.gpsimd.memset(ident[:, :], 0.0).then_inc(const_ready, 1)
            nc.gpsimd.memset(comp_diag[:, :, :], 0.0).then_inc(comp_zeroed, 1)
            pool.wait_ge(const_ready, 1)
            nc.gpsimd.affine_select(out=ident[:, :], in_=ident[:, :], compare_op=ALU.not_equal, fill=1.0,
                                    base=0, pattern=[[-1, P]], channel_multiplier=1).then_inc(const_ready, 1)
            IMPRECISE = dict(allow_small_or_imprecise_dtypes=True)
            nc.gpsimd.iota(iota_win[:, :], [[1, WIN]], base=0, channel_multiplier=0, **IMPRECISE).then_inc(const_ready, 1)
            nc.gpsimd.iota(iota_wide[:, :], [[1, WIDE]], base=0, channel_multiplier=0, **IMPRECISE).then_inc(const_ready, 1)
            nc.gpsimd.iota(wide_starts[:, :], [[WIDE, WIDES]], base=0, channel_multiplier=0, **IMPRECISE).then_inc(const_ready, 1)
            nc.gpsimd.iota(iota_col[:, :], [[1, 1]], base=0, channel_multiplier=1, **IMPRECISE).then_inc(const_ready, 1)
            for q in range(4):
                pool.wait_ge(const_ready, 6 + q)
                nc.gpsimd.iota(relation_col[32 * q:32 * q + 32, :], [[1, 1]], base=0, channel_multiplier=1,
                               **IMPRECISE).then_inc(const_ready, 1)
            pool.wait_ge(const_ready, 10)
            nc.gpsimd.memset(zero_col[:, :], 0.0).then_inc(const_ready, 1)
            nc.gpsimd.memset(ln_eps_col[:, :], LN_EPS).then_inc(const_ready, 1)

            wide = read_flag(pool, ENGINE.Pool)
            for r, table in enumerate((x, x1_table)):
                if r == 1:
                    pool.wait_ge(x1_out[0], 16 * (CHUNKS // 2 + 1))
                    pool.wait_ge(x1_out[1], 16 * (CHUNKS // 2))
                with pool.If(wide < 1):
                    with pool.Fori(0, GROUPS // RING) as i:
                        for s in range(RING):
                            wait_alone(pool, slots_ready[r], i * RING + s + 1)
                            for j in range(s * GROUP, (s + 1) * GROUP):
                                pool.indirect_dma_start(
                                    gathered[:, j, :], None, table[:, :],
                                    bass.IndirectOffsetOnAxis(src_slots[:, j:j + 1], 0)).then_inc(gather_in[r][s], 16)
                with pool.Else():
                    with pool.Fori(0, T) as t:
                        wait_alone(pool, wide_slot[r], t + 1)
                        pool.indirect_dma_start(
                            gathered[:, 0, :], None, table[:, :],
                            bass.IndirectOffsetOnAxis(src_slots[:, 0:1], 0)).then_inc(wide_gather[r], 16)

        @block.scalar
        def _(act):
            act.sem_inc(agg_relu, 2)
            act.sem_inc(x1_t_ready, 2)
            act.sem_inc(hidden_ready, 4)
            act.wait_ge(comp_zeroed, 1)
            for q in range(4):
                act.dma_start(comp_diag[32 * q:32 * q + 32, q, :], w_comp[:, :]).then_inc(comp_in, 16)
            act.dma_start(w_base[:, :, :], weight.rearrange("b i o -> i b o")).then_inc(weights_in, 16)
            act.dma_start(w1_sb[:, :], w1[:, :]).then_inc(weights_in, 16)
            act.dma_start(w2_sb[:, :, :], w2.rearrange("(j p) o -> p j o", p=P)).then_inc(weights_in, 16)
            act.dma_start(bias0_col[:, :], bias0.rearrange("(p a) -> p a", a=1)).then_inc(weights_in, 16)
            act.dma_start(b2_col[:, :], b2.rearrange("(p a) -> p a", a=1)).then_inc(weights_in, 16)
            for col, vec in ((b1_col, b1), (gamma_col, gamma), (beta_col, beta)):
                for j in range(2):
                    act.dma_start(col[:, j:j + 1],
                                  vec[j * P:(j + 1) * P].rearrange("(p a) -> p a", a=1)).then_inc(weights_in, 16)
            act.dma_start(eps_col[:, :], eps.partition_broadcast(P)).then_inc(weights_in, 16)

            wide = read_flag(act, ENGINE.Activation)

            def zero_sums():
                act.wait_ge(const_ready, 12)
                for b in range(B + 1):
                    nc.scalar.activation(sums[:, b, :], zero_col[:, 0:1].to_broadcast([P, NP]), ACT.Copy).then_inc(zeroed, 1)

            def copy_slots(r, g, s):
                act.wait_ge(group_mm[r], g + 1)
                nc.scalar.activation(src_slots[:, s * GROUP:(s + 1) * GROUP],
                                     src_t[:, bass.ds(g * GROUP, GROUP)], ACT.Copy).then_inc(slots_ready[r], 1)

            def edge_round(r):
                with act.If(wide < 1):
                    for s in range(RING):
                        copy_slots(r, s, s)
                    if r == 0:
                        zero_sums()
                    with act.Fori(1, GROUPS // RING) as i:
                        for s in range(RING):
                            copy_slots(r, i * RING + s, s)
                with act.Else():
                    if r == 0:
                        zero_sums()
                    with act.Fori(0, T) as t:
                        act.wait_ge(wide_tile[r], t + 1)
                        nc.scalar.activation(src_slots[:, 0:1], src_t[:, bass.ds(t, 1)], ACT.Copy).then_inc(wide_slot[r], 1)

            edge_round(0)

            def relu_agg(k, s, n):
                act.wait_ge(agg_mm, k + 1)
                act.wait_ge(agg_turned, k + 1)
                nc.scalar.activation(layer_stage[:, s, 0:n], psum[:, s, 0:n], ACT.Relu,
                                     bias=bias0_col[:, 0:1]).then_inc(agg_relu, 1)

            def deviations(r):
                def stage(k, s, n):
                    c, rows = len(tiles_of(n)), min(n, P)
                    act.wait_ge(ln_var[r], k * CT + c)
                    nc.scalar.activation(ln_std[0:rows, s, 0:c], ln_mv[0:rows, s, 0:c, 1], ACT.Sqrt,
                                         bias=ln_eps_col[0:rows, 0:1]).then_inc(ln_std_ready[r], 1)
                return stage

            def keep_x1(k, s, n):
                act.wait_ge(x1_turned, k + 1)
                nc.scalar.activation(x1_t[:, span(k, n)], psum[:, 4 + s, 0:n], ACT.Copy).then_inc(x1_t_ready, 1)

            act.wait_ge(weights_in, 16 * 12)
            chunk_pipeline(act, relu_agg, deviations(0), keep_x1)

            edge_round(1)

            def keep_hidden(k, s, n):
                act.wait_ge(hidden_mm, k + 1)
                for j in range(2):
                    nc.scalar.activation(hidden[:, j, span(k, n)], psum[:, 2 * s + j, 0:n], ACT.Identity,
                                         bias=b1_col[:, j:j + 1]).then_inc(hidden_ready, 1)

            chunk_pipeline(act, keep_hidden)
            act.wait_ge(bn_var, 2)
            nc.scalar.activation(bn_std[:, :], bn_mv[:, :, 1], ACT.Sqrt, bias=ln_eps_col[:, 0:1]).then_inc(bn_std_ready, 1)
            act.wait_ge(bn_ready, 1)

            def relu_hidden(k, s, n):
                act.wait_ge(out_mm, k + 1)
                for j in range(2):
                    nc.scalar.activation(relu_stage[:, s, j, 0:n], hidden[:, j, span(k, n)], ACT.Relu,
                                         bias=bn_shift[:, j:j + 1], scale=bn_scale[:, j:j + 1]).then_inc(relu_ready, 1)

            chunk_pipeline(act, relu_hidden, deviations(1))

        @block.tensor
        def _(pe):
            pe.sem_inc(coef_mm, 2)
            pe.sem_inc(group_mm[0], RING)
            pe.sem_inc(agg_turned, 2)
            pe.sem_inc(out_mm, 2)
            pe.sem_inc(out_turned, 2)

            def turn(rows, bank):
                for q in range(4):
                    last = nc.tensor.transpose(psum[:, bank, q * TQ:(q + 1) * TQ], rows[:, q, :], ident[0:TQ, 0:TQ])
                return last

            pe.wait_ge(const_ready, 2)
            pe.wait_ge(srcf_ready, 1)
            turn(srcf_rows, 0).then_inc(src_turned, 1)
            pe.wait_ge(rows_ready, 1)
            turn(rel_rows, 1)
            turn(dstf_rows, 2)
            turn(norm_rows, 3)
            for bank, col in ((4, base_col), (5, span_col)):
                for q in range(4):
                    last = nc.tensor.matmul(psum[0:1, bank, q * TQ:(q + 1) * TQ], col[:, q:q + 1],
                                            ident[0:TQ, 0:TQ], start=True, stop=True)
            last.then_inc(turned, 1)

            pe.wait_ge(comp_in, 64)
            with pe.Fori(0, PIECES // 2) as i:
                for s in range(2):
                    pe.wait_ge(hot_built, i * 2 + s + 3)
                    pe.wait_ge(coef_ready, i * 2 + s + 1)
                    for j in range(PQ):
                        last = nc.tensor.matmul(psum[:, 6 + s, j * 4 * B:(j + 1) * 4 * B],
                                                etype_hot[:, s, j * P:(j + 1) * P],
                                                comp_diag[:, :, :].rearrange("p q b -> p (q b)"), start=True, stop=True)
                    last.then_inc(coef_mm, 1)

            wide = read_flag(pe, ENGINE.PE)

            def edge_round(r):
                with pe.If(wide < 1):
                    with pe.Fori(0, GROUPS // RING) as i:
                        for s in range(RING):
                            g = i * RING + s
                            pe.wait_ge(gather_in[r][s], i * 16 * GROUP + 16 * GROUP)
                            if r == 0:
                                pe.wait_ge(attrs_in[s], i * 32 + 32)
                                pe.wait_ge(select_ready, g + 1)
                            else:
                                pe.wait_ge(hot_ready[r], g + 1)
                            pe.wait_ge(added[r], g * GROUP + GROUP + 1)
                            for j in range(GROUP):
                                ps = tile_psum(s % 2, j)
                                if r == 0:
                                    nc.tensor.matmul(ps[:, 0:B, :], gathered[:, s * GROUP + j, :],
                                                     weighted[:, s % 2, j, :, :], start=True, stop=True)
                                    last = nc.tensor.matmul(ps[:, B, :], attrs[:, s * GROUP + j, :],
                                                            hot[:, s % 2, j, :], start=True, stop=True)
                                else:
                                    last = nc.tensor.matmul(ps[:, B, :], gathered[:, s * GROUP + j, :],
                                                            hot[:, s % 2, j, :], start=True, stop=True)
                            last.then_inc(group_mm[r], 1)
                with pe.Else():
                    with pe.Fori(0, T) as t:
                        wait_alone(pe, wide_gather[r], t * 16 + 16)
                        if r == 0:
                            wait_alone(pe, wide_attr, t * 16 + 16)
                        with pe.Fori(0, WIDES) as w:
                            if r == 0:
                                pe.wait_ge(wide_select, t * WIDES + w + 1)
                                for h in range(B // 4):
                                    nc.tensor.matmul(psum[:, h, 0:4 * WIDE], gathered[:, 0, :],
                                                     wide_weighted[:, 4 * h:4 * h + 4, :], start=True, stop=True)
                                last = nc.tensor.matmul(wide_psum(B), attrs[:, 0, :], wide_hot_sb[:, :],
                                                        start=True, stop=True)
                            else:
                                pe.wait_ge(wide_hot[r], t * WIDES + w + 1)
                                last = nc.tensor.matmul(wide_psum(B), gathered[:, 0, :], wide_hot_sb[:, :],
                                                        start=True, stop=True)
                            last.then_inc(wide_mm[r], 1)

            edge_round(0)
            pe.wait_ge(round_done[0], 1)

            def turn_chunk(bank, source, n, tiles_in):
                for i, rows in tiles_of(n):
                    if tiles_in == "feature":
                        last = nc.tensor.transpose(psum[0:rows, bank, i * P:(i + 1) * P],
                                                   source[:, i * P:i * P + rows], ident[:, :])
                    else:
                        last = nc.tensor.transpose(psum[:, bank, i * P:i * P + rows],
                                                   source[0:rows, i, :], ident[0:rows, 0:rows])
                return last

            def through_bases(k, s, n):
                pe.wait_ge(agg_relu, k + 1)
                for b in range(B):
                    last = nc.tensor.matmul(psum[:, s, 0:n], w_base[:, b, :], sums[:, b, span(k, n)],
                                            start=(b == 0), stop=(b == B - 1))
                last.then_inc(agg_mm, 1)

            def turn_agg(k, s, n):
                pe.wait_ge(agg_relu, k + 3)
                pe.wait_ge(x1_ready, k * CT + CT)
                turn_chunk(2 + s, layer_stage[:, s, :], n, "feature").then_inc(agg_turned, 1)

            def turn_x1(k, s, n):
                pe.wait_ge(x1_ready, (k + 2) * CT + len(tiles_of(n)))
                pe.wait_ge(x1_t_ready, k + 1)
                turn_chunk(4 + s, node_stage[:, s, :, :], n, "node").then_inc(x1_turned, 1)

            pe.wait_ge(weights_in, 16 * 12)
            chunk_pipeline(pe, through_bases, turn_agg, turn_x1)

            pe.wait_ge(x1_t_ready, CHUNKS + 3)
            pe.sem_inc(group_mm[1], RING)
            edge_round(1)

            def into_hidden(k, s, n):
                pe.wait_ge(rst_ready, k + 1)
                pe.wait_ge(hidden_ready, k * 2 + 2)
                for j in range(2):
                    last = nc.tensor.matmul(psum[:, 2 * s + j, 0:n], w1_sb[:, j * P:(j + 1) * P],
                                            sums[:, B, span(k, n)], start=True, stop=True)
                last.then_inc(hidden_mm, 1)

            chunk_pipeline(pe, into_hidden)
            pe.wait_ge(bn_ready, 1)

            def into_out(k, s, n):
                pe.wait_ge(relu_ready, k * 2 + 2)
                pe.wait_ge(out_t_ready, k + 1)
                for j in range(2):
                    last = nc.tensor.matmul(psum[:, s, 0:n], w2_sb[:, j, :], relu_stage[:, s, j, 0:n],
                                            start=(j == 0), stop=(j == 1))
                last.then_inc(out_mm, 1)

            def turn_out(k, s, n):
                pe.wait_ge(out_t_ready, k + 3)
                pe.wait_ge(out_ready, k * CT + CT)
                turn_chunk(2 + s, layer_stage[:, s, :], n, "feature").then_inc(out_turned, 1)

            chunk_pipeline(pe, into_out, turn_out)

        @block.vector
        def _(dve):
            steps = [0]

            def link(instruction):
                steps[0] += 1
                instruction.then_inc(prep, 1)
                dve.wait_ge(prep, steps[0])

            dve.sem_inc(hot_built, 2)
            dve.sem_inc(coef_ready, 2)
            dve.sem_inc(added[0], 2 * GROUP + 1)
            dve.sem_inc(added[1], 2 * GROUP + 1)
            dve.sem_inc(wide_add[0], 1)
            dve.sem_inc(wide_add[1], 1)
            dve.sem_inc(wide_tile[0], 1)
            dve.sem_inc(x1_ready, 2 * CT)
            dve.sem_inc(out_t_ready, 2)
            dve.sem_inc(out_ready, 2 * CT)

            dve.wait_ge(src_in, 16 * 5)
            nc.vector.tensor_copy(srcf_rows[:, :, :], src_rows[:, :, :]).then_inc(srcf_ready, 1)
            dve.wait_ge(rows_in, 16 * 10)
            link(nc.vector.tensor_copy(dstf_rows[:, :, :], dst_rows[:, :, :]))
            link(nc.vector.tensor_reduce(base_col[:, :], dstf_rows[:, :, :], AX_X, ALU.min))
            nc.vector.tensor_tensor(rel_rows[:, :, :], dstf_rows[:, :, :],
                                    base_col[:, :].unsqueeze(2).to_broadcast([TQ, 4, P]), ALU.subtract)
            link(nc.vector.tensor_reduce(high_col[:, :], dstf_rows[:, :, :], AX_X, ALU.max))
            nc.vector.tensor_tensor(span_col[:, :], high_col[:, :], base_col[:, :], ALU.subtract).then_inc(rows_ready, 1)
            dve.wait_ge(src_turned, 1)
            nc.vector.tensor_copy(src_t[:, :], psum[:, 0, 0:T]).then_inc(src_t_ready, 1)
            dve.wait_ge(turned, 1)
            link(nc.vector.tensor_reduce(span_max[0:1, :], psum[0:1, 5, 0:T], AX_X, ALU.max))
            nc.vector.tensor_scalar(wide_flag[0:1, :], span_max[0:1, :], float(WIN), None, ALU.is_ge)
            nc.vector.tensor_copy(base_row[0:1, :], psum[0:1, 4, 0:T])
            nc.vector.tensor_copy(norm_t[:, :], psum[:, 3, 0:T])
            nc.vector.tensor_copy(rel_t[:, :], psum[:, 1, 0:T])
            nc.vector.tensor_copy(dst_t[:, :], psum[:, 2, 0:T])
            dve.wait_ge(const_ready, 12)
            link(nc.vector.tensor_scalar(own_col[:, :], iota_col[:, :], float(P - FRESH), None, ALU.is_ge))
            for cols in (rel_t, dst_t):
                last_col = cols[:, T - 1:T]
                link(nc.vector.tensor_scalar(last_col, last_col, 1.0, own_col[:, 0:1], ALU.add, ALU.mult))
                link(nc.vector.tensor_scalar(last_col, last_col, -1.0, None, ALU.add))
            dve.sem_inc(flag_ready, 1)

            coef_view = coef[:, :, :].rearrange("p (q t) b -> p t q b", q=4)
            norm_view = norm_t[:, :].rearrange("p (q t) -> p t q", q=4)

            def relation_hot(i, m, s):
                dve.wait_ge(etype_in[s], i * 128 + 128)
                dve.wait_ge(coef_mm, m + 1)
                nc.vector.tensor_scalar(etype_hot[:, s, :], etype_bc[:, s, :], relation_col[:, 0:1], None,
                                        ALU.is_equal).then_inc(hot_built, 1)

            def coefficients(m, s):
                dve.wait_ge(coef_mm, m + 3)
                nc.vector.tensor_tensor(
                    coef_view[:, bass.ds(m * PQ, PQ), :, :],
                    psum[:, 6 + s, 0:PQ * 4 * B].rearrange("p (t q b) -> p t q b", q=4, b=B),
                    norm_view[:, bass.ds(m * PQ, PQ), :].unsqueeze(3).to_broadcast([P, PQ, 4, B]),
                    ALU.mult).then_inc(coef_ready, 1)

            relation_hot(0, 0, 0)
            relation_hot(0, 1, 1)
            with dve.Fori(0, PIECES // 2 - 1) as i:
                for s in range(2):
                    coefficients(i * 2 + s, s)
                    relation_hot(i + 1, i * 2 + 2 + s, s)
            for s in range(2):
                coefficients(PIECES - 2 + s, s)
            dve.wait_ge(coef_ready, PIECES + 2)
            dve.wait_ge(zeroed, B + 1)

            wide = read_flag(dve, ENGINE.DVE)

            def select(r, g, s):
                dve.wait_ge(group_mm[r], g + 3)
                nc.vector.tensor_tensor(
                    hot[:, s, :, :], rel_t[:, bass.ds(g * GROUP, GROUP)].unsqueeze(2).to_broadcast([P, GROUP, WIN]),
                    iota_win[:, :].unsqueeze(1).to_broadcast([P, GROUP, WIN]), ALU.is_equal).then_inc(hot_ready[r], 1)
                if r == 0:
                    dve.wait_ge(hot_ready[r], g + 1)
                    nc.vector.tensor_tensor(
                        weighted[:, s, :, :, :], hot[:, s, :, :].unsqueeze(2).to_broadcast([P, GROUP, B, WIN]),
                        coef[:, bass.ds(g * GROUP, GROUP), :].unsqueeze(3).to_broadcast([P, GROUP, B, WIN]),
                        ALU.mult).then_inc(select_ready, 1)

            def add(r, g, s):
                bases = nc.values_load_multi_w_load_instructions(
                    base_row[0:1, bass.ds(g * GROUP, GROUP)], engines=(ENGINE.DVE,), min_val=0, max_val=N - 1,
                    skip_runtime_bounds_check_because="bases are node numbers")[1]
                dve.wait_ge(group_mm[r], g + RING + 1)
                for j in range(GROUP):
                    rows = slice(0, B + 1) if r == 0 else slice(B, B + 1)
                    window = sums[:, rows, bass.ds(bases[j], WIN)]
                    dve.wait_ge(added[r], g * GROUP + 2 * GROUP + 1 + j)
                    nc.vector.tensor_tensor(window, tile_psum(s, j)[:, rows, :], window, ALU.add).then_inc(added[r], 1)

            def edge_round(r):
                with dve.If(wide < 1):
                    select(r, 0, 0)
                    with dve.Fori(0, GROUPS // 2 - 1) as i:
                        for s in range(2):
                            select(r, i * 2 + s + 1, 1 - s)
                            add(r, i * 2 + s, s)
                    select(r, GROUPS - 1, 1)
                    add(r, GROUPS - 2, 0)
                    add(r, GROUPS - 1, 1)
                    dve.wait_ge(added[r], T + 2 * GROUP + 1)
                with dve.Else():
                    adds = 2 if r == 0 else 1
                    with dve.Fori(0, T) as t:
                        with dve.Fori(0, WIDES) as w:
                            j = t * WIDES + w
                            dve.wait_ge(wide_add[r], j * adds + 1)
                            nc.vector.tensor_scalar(wide_hot_sb[:, :], iota_wide[:, :], wide_starts[:, bass.ds(w, 1)],
                                                    dst_t[:, bass.ds(t, 1)], ALU.add, ALU.is_equal).then_inc(wide_hot[r], 1)
                            if r == 0:
                                dve.wait_ge(wide_hot[r], j + 1)
                                nc.vector.tensor_tensor(
                                    wide_weighted[:, :, :], wide_hot_sb[:, :].unsqueeze(1).to_broadcast([P, B, WIDE]),
                                    coef[:, bass.ds(t, 1), :].rearrange("p t b -> p (t b)").unsqueeze(2)
                                    .to_broadcast([P, B, WIDE]), ALU.mult).then_inc(wide_select, 1)
                            dve.wait_ge(wide_mm[r], j + 1)
                            if r == 0:
                                window = sums[:, 0:B, bass.ds(w * WIDE, WIDE)].rearrange("p (h b) n -> p h b n", b=4)
                                nc.vector.tensor_tensor(
                                    window, psum[:, 0:B // 4, 0:4 * WIDE].rearrange("p h (b n) -> p h b n", b=4),
                                    window, ALU.add).then_inc(wide_add[r], 1)
                            window = sums[:, B, bass.ds(w * WIDE, WIDE)]
                            nc.vector.tensor_tensor(window, wide_psum(B), window, ALU.add).then_inc(wide_add[r], 1)
                        dve.sem_inc(wide_tile[r], 1)
                    dve.wait_ge(wide_add[r], T * WIDES * adds + 1)
                dve.sem_inc(round_done[r], 1)

            edge_round(0)

            def statistics(r, k, s, n, source):
                for i, rows in tiles_of(n):
                    nc.vector.bn_stats(ln_part[0:rows, s, i, :], source(i, rows)).then_inc(ln_stats[r], 1)
                wait_alone(dve, ln_stats[r], k * CT + len(tiles_of(n)))
                for i, rows in tiles_of(n):
                    nc.vector.bn_aggr(ln_mv[0:rows, s, i, :], ln_part[0:rows, s, i, :]).then_inc(ln_var[r], 1)

            def normalise(r, k, s, n, source, target, signal):
                c, top = len(tiles_of(n)), min(n, P)
                dve.wait_ge(ln_std_ready[r], k + 1)
                nc.vector.reciprocal(ln_rstd[0:top, s, 0:c], ln_std[0:top, s, 0:c]).then_inc(ln_rstd_ready[r], 1)
                dve.wait_ge(ln_rstd_ready[r], k + 1)
                for i, rows in tiles_of(n):
                    nc.vector.tensor_scalar(target(i, rows), source(i, rows), ln_mv[0:rows, s, i, 0:1],
                                            ln_rstd[0:rows, s, i:i + 1], ALU.subtract, ALU.mult).then_inc(signal, 1)

            def residual(k, s, n):
                dve.wait_ge(agg_turned, k + 3)
                c, rows = len(tiles_of(n)), min(n, P)
                both = node_stage[0:rows, s, 0:c, :]
                nc.vector.tensor_tensor(both, psum[0:rows, 2 + s, 0:c * P].rearrange("p (t f) -> p t f", f=F), both,
                                        ALU.add).then_inc(res_ready[0], 1)
                dve.wait_ge(res_ready[0], k + 1)
                statistics(0, k, s, n, lambda i, rows: node_stage[0:rows, s, i, :])

            def first_residual(k, s, n):
                dve.wait_ge(x_in[s], (k - s) * 8 + 16)
                residual(k, s, n)

            def first_norm(k, s, n):
                tile = lambda i, rows: node_stage[0:rows, s, i, :]
                normalise(0, k, s, n, tile, tile, x1_ready)

            chunk_pipeline(dve, first_residual, first_norm)

            dve.wait_ge(x1_ready, 2 * CT + CHUNKS * CT + 1)
            dve.sem_inc(wide_tile[1], 1)
            edge_round(1)

            link(nc.vector.tensor_scalar(one_eps[:, :], eps_col[:, :], 1.0, None, ALU.add))
            dve.wait_ge(x1_t_ready, CHUNKS + 3)

            def rst(k, s, n):
                total = sums[:, B, span(k, n)]
                nc.vector.scalar_tensor_tensor(total, x1_t[:, span(k, n)], one_eps[:, 0:1], total,
                                               ALU.mult, ALU.add).then_inc(rst_ready, 1)

            chunk_pipeline(dve, rst)

            def hidden_stats(k, s, n):
                dve.wait_ge(hidden_ready, k * 2 + 6)
                for j in range(2):
                    nc.vector.bn_stats(bn_part[:, j, bass.ds(k, 1), :].rearrange("p a c -> p (a c)"),
                                       hidden[:, j, span(k, n)]).then_inc(bn_step, 1)

            chunk_pipeline(dve, hidden_stats)
            dve.wait_ge(bn_step, 2 * (CHUNKS + 1))
            for j in range(2):
                nc.vector.bn_aggr(bn_mv[:, j, :], bn_part[:, j, :, :].rearrange("p k c -> p (k c)")).then_inc(bn_var, 1)
            dve.wait_ge(bn_std_ready, 1)
            link(nc.vector.reciprocal(bn_rstd[:, :], bn_std[:, :]))
            link(nc.vector.tensor_tensor(bn_scale[:, :], bn_rstd[:, :], gamma_col[:, :], ALU.mult))
            link(nc.vector.tensor_tensor(bn_ms[:, :], bn_mv[:, :, 0], bn_scale[:, :], ALU.mult))
            nc.vector.tensor_tensor(bn_shift[:, :], beta_col[:, :], bn_ms[:, :], ALU.subtract).then_inc(bn_ready, 1)

            def second_residual(k, s, n):
                dve.wait_ge(out_mm, k + 3)
                dve.wait_ge(out_turned, k + 1)
                nc.vector.scalar_tensor_tensor(layer_stage[:, s, 0:n], psum[:, s, 0:n], b2_col[:, 0:1],
                                               x1_t[:, span(k, n)], ALU.add, ALU.add).then_inc(out_t_ready, 1)

            def out_tile(s, i, rows):
                return psum[0:rows, 2 + s, i * P:(i + 1) * P]

            def second_stats(k, s, n):
                dve.wait_ge(out_turned, k + 3)
                statistics(1, k, s, n, lambda i, rows: out_tile(s, i, rows))

            def second_norm(k, s, n):
                normalise(1, k, s, n, lambda i, rows: out_tile(s, i, rows),
                          lambda i, rows: out_stage[0:rows, bass.ds(k * CT + i, 1), :].rearrange("p t f -> p (t f)"),
                          out_ready)

            chunk_pipeline(dve, second_residual, second_stats, second_norm)


_INS = ['x', 'src', 'dst', 'edge_attr_128', 'edge_type_32', 'edge_weight1', 'L0_gnn_weight', 'L0_gnn_w_comp',
        'L0_gnn_bias_param', 'L1_gnn_eps', 'L1_gnn_W1', 'L1_gnn_b1', 'L1_gnn_gamma', 'L1_gnn_beta', 'L1_gnn_W2',
        'L1_gnn_b2']


def kernel(**inputs):
    import numpy as _np
    import concourse.bacc as _bacc
    from concourse import mybir as _mybir
    from concourse.bass_utils import run_bass_kernel_spmd as _run

    nc = _bacc.Bacc("TRN2", target_bir_lowering=False, num_devices=1)
    arrays, args = {}, []
    for name in _INS:
        a = _np.ascontiguousarray(inputs[name])
        if name == 'edge_weight1':
            a = a.reshape(-1)
        arrays[f"in_{name}_dram"] = a
        args.append(nc.dram_tensor(f"in_{name}_dram", a.shape, _mybir.dt.from_np(a.dtype), kind="ExternalInput").ap())
    args.append(nc.dram_tensor("out_0_dram", inputs['x'].shape, _mybir.dt.float32, kind="ExternalOutput").ap())
    gnn_resnorm_kernel(nc, *args)
    r = _run(nc, [arrays], core_ids=[0])
    return r.results[0]["out_0_dram"]
```

```python
from contextlib import ExitStack

import concourse.bass as bass
from concourse import mybir

F32 = mybir.dt.float32
F16 = mybir.dt.float16
BF16 = mybir.dt.bfloat16
I32 = mybir.dt.int32
ALU = mybir.AluOpType
ACT = mybir.ActivationFunctionType
AX_X = mybir.AxisListType.X
AX_XY = mybir.AxisListType.XY
ENGINE = mybir.EngineType

P = 128
WIN = 16
GROUP = 8
RING = 4
SPREAD = 80
BLOCK = 4
CHUNK = 512
LN_EPS = 1e-5
BN_EPS = 1e-5


def gnn_resnorm_kernel(nc, x, src, dst, edge_attr, etype, norm, weight, w_comp, bias0,
                       eps, w1, b1, gamma, beta, w2, b2, out):
    N, F = x.shape
    E = src.shape[0]
    B = weight.shape[0]
    R = w_comp.shape[0]
    H = w1.shape[1]
    assert F == P and H == 2 * P and R == 32

    T = -(-E // P)
    FRESH = E - (T - 1) * P
    TQ = T // 4
    assert T == 4 * TQ and T % (GROUP * RING) == 0 and 0 < FRESH <= P
    GROUPS = T // GROUP
    NP = N + WIN - 1
    WIDE = 125
    WIDES = -(-N // WIDE)
    assert WIDES * WIDE <= NP and 4 * WIDE <= 512
    CHUNKS = N // CHUNK
    REST = N - CHUNKS * CHUNK
    CT = CHUNK // P
    assert CHUNKS % 2 == 0 and 0 < REST <= P
    PQ = 13
    PIECES = TQ // PQ
    assert TQ % PQ == 0 and PIECES % 4 == 0 and PQ * 4 * B <= 512 and PQ >= GROUP

    HIGHS = -(-N // P)
    KEYS = HIGHS * WIN
    FAR = 4096.0
    BLOCKS = GROUPS // BLOCK
    ROW = F + P // 2
    assert GROUP * P <= 2048 and KEYS <= 512 and FAR > KEYS and BLOCKS % 2 == 1
    assert GROUPS == BLOCK * BLOCKS and RING == BLOCK and BLOCK * SPREAD <= 512

    x_table = nc.dram_tensor("x_table", (N, ROW), F32, kind="Internal").ap()
    relations = nc.dram_tensor("relations", (4, TQ, P), F16, kind="Internal").ap()
    adjacency = nc.dram_tensor("adjacency", (P, GROUPS, HIGHS * SPREAD), F16, kind="Internal").ap()
    x1_table = nc.dram_tensor("x1_table", (N, F), F32, kind="Internal").ap()

    with ExitStack() as ctx:
        def sb(name, shape, dt=F32):
            return ctx.enter_context(nc.sbuf_tensor(name, shape, dt))

        def sem(name):
            return ctx.enter_context(nc.semaphore(name))

        attrs = sb("attrs", [P, 2 * GROUP, F])
        weighted = sb("weighted", [P, 2, GROUP, B, WIN])
        weighted_flat = weighted[:, :, :, :, :].rearrange("p s t b n -> p (s t b n)")
        rows_a = attrs[0:TQ, :, :].rearrange("p (i q) f -> p i q f", q=4)
        rows_b = weighted_flat[0:TQ, :].rearrange("p (i q f) -> p i q f", q=4, f=F)
        src_rows, high_rows, dst_rows = rows_a[:, 0].bitcast(I32), rows_a[:, 1].bitcast(I32), rows_a[:, 2].bitcast(I32)
        srcf_rows, dstf_rows, rel_rows, norm_rows, key_rows = rows_a[:, 3], rows_b[:, 0], rows_b[:, 1], rows_b[:, 2], rows_b[:, 3]
        base_col = sb("base_col", [TQ, 4])
        high_col = sb("high_col", [TQ, 4])
        span_col = sb("span_col", [TQ, 4])
        src_t = sb("src_t", [P, T])
        rel_t = sb("rel_t", [P, T])
        norm_t = sb("norm_t", [P, T])
        key_t = sb("key_t", [P, T])
        base_row = sb("base_row", [1, GROUPS, 2 * GROUP], I32)
        flags = sb("flags", [1, 8])
        wide_flag = sb("wide_flag", [1, 1], I32)
        coef = sb("coef", [P, T, B])
        adj_ring = sb("adj_ring", [P, RING, HIGHS * SPREAD], F16)
        adj_flat = adj_ring[:, :, :].rearrange("p s n -> p (s n)")
        assert 4 * PQ * P + 2 * T <= RING * HIGHS * SPREAD and B * WIDE <= B * F
        dst_t = adj_flat[:, 4 * PQ * P:4 * PQ * P + 2 * T].bitcast(F32)
        etype_bc = adj_flat[:, 0:4 * PQ * P].rearrange("p (s e) -> p s e", s=4)
        coef_flat = coef[:, :, :].rearrange("p t b -> p (t b)")
        etype_rows = coef_flat[0:TQ, 0:4 * P].bitcast(I32).rearrange("p (q e) -> p q e", q=4)
        etype16_rows = coef_flat[0:TQ, 4 * P:6 * P].bitcast(F16).rearrange("p (q e) -> p q e", q=4)
        etype_hot_flat = sb("etype_hot", [P, 2 * PQ * P])
        etype_hot = etype_hot_flat[:, :].bitcast(BF16).rearrange("p (s e) -> p s e", s=4)
        relation_col = sb("relation_col", [P, 1])
        comp_diag = sb("comp_diag", [P, 4, B])
        comp_left = sb("comp_left", [P, 4, B])
        comp_parts = sb("comp_parts", [P, 3, 4 * B], BF16)
        ident = sb("ident", [P, P])
        ident16 = sb("ident16", [P, P], F16)
        iota_key = sb("iota_key", [P, KEYS], F16)
        iota_win = sb("iota_win", [P, WIN])
        iota_wide = sb("iota_wide", [P, WIDE])
        wide_starts = sb("wide_starts", [P, WIDES])
        iota_col = sb("iota_col", [P, 1])
        own_col = sb("own_col", [P, 1])
        zero_col = sb("zero_col", [P, 1])
        ln_eps_col = sb("ln_eps_col", [P, 1])
        w_base = weighted_flat[:, 0:B * F].rearrange("p (b o) -> p b o", b=B)
        w1_sb = weighted_flat[:, B * F:B * F + H]
        w2_sb = weighted_flat[:, B * F + H:B * F + 2 * H].rearrange("p (j o) -> p j o", j=2)
        bias0_col = sb("bias0_col", [P, 1])
        b1_col = sb("b1_col", [P, 2])
        gamma_col = sb("gamma_col", [P, 2])
        beta_col = sb("beta_col", [P, 2])
        b2_col = sb("b2_col", [P, 1])
        eps_col = sb("eps_col", [P, 1])
        one_eps = sb("one_eps", [P, 1])
        sums_flat = sb("sums_flat", [P, (B + 1) * NP + SPREAD])
        sums = sums_flat[:, 0:(B + 1) * NP].rearrange("p (b n) -> p b n", n=NP)
        key_hot = etype_hot_flat[:, 0:GROUP * KEYS].bitcast(F16).rearrange("p (s t n) -> p s t n", s=2, n=KEYS)
        x1_t = etype_hot_flat[:, 0:N]
        gathered = sb("gathered", [P, RING * GROUP, ROW])
        gathered_flat = gathered[:, :, :].rearrange("p t f -> p (t f)")
        src_slots = sb("src_slots", [P, RING * GROUP], I32)
        hot = sb("hot", [P, 2, GROUP, WIN])
        wide_hot_sb = weighted_flat[:, B * F + 2 * H:B * F + 2 * H + WIDE]
        wide_weighted = weighted_flat[:, 0:B * WIDE] \
            .rearrange("p (b n) -> p b n", n=WIDE)
        node_stage = attrs[:, 0:2 * CT, :].rearrange("p (s t) f -> p s t f", s=2)
        layer_stage = attrs[:, 2 * CT:4 * CT, :].rearrange("p (s t) f -> p s (t f)", s=2)
        out_stage = gathered_flat[:, 0:HIGHS * F].rearrange("p (t f) -> p t f", f=F)
        x1_parts = gathered_flat[:, 0:HIGHS * 3 * F // 2].bitcast(BF16).rearrange("p (h c f) -> p h c f", c=3, f=F)
        left = coef[:, 0:2 * CHUNK // B, :].rearrange("p (s t) b -> p s (t b)", s=2).rearrange("p s (t f) -> p s t f", f=F)
        adj_blocks = [buffer.rearrange("p (g h n) -> p g h n", g=BLOCK, n=SPREAD) for buffer in
                      (adj_flat, sums_flat[:, 0:BLOCK * HIGHS * SPREAD // 2].bitcast(F16))]
        hidden = sums[:, 0:2, 0:N]
        relu_stage = sums[:, 2:4, 0:2 * CHUNK].rearrange("p s (j n) -> p s j n", j=2)
        bn_part = sb("bn_part", [P, 2, CHUNKS + 1, 6])
        bn_mv = sb("bn_mv", [P, 2, 2])
        bn_std = sb("bn_std", [P, 2])
        bn_rstd = sb("bn_rstd", [P, 2])
        bn_scale = sb("bn_scale", [P, 2])
        bn_ms = sb("bn_ms", [P, 2])
        bn_shift = sb("bn_shift", [P, 2])
        ln_part = sb("ln_part", [P, 2, CT, 6])
        ln_mv = sb("ln_mv", [P, 2, CT, 2])
        ln_std = sb("ln_std", [P, 2, CT])
        ln_rstd = sb("ln_rstd", [P, 2, CT])

        psum = ctx.enter_context(nc.psum_tensor("psum", [P, 8, 512], F32))

        def tile_psum(slot, i):
            c = (i % 3) * (B + 1) * WIN
            return psum[:, 3 * slot + i // 3, c:c + (B + 1) * WIN].rearrange("p (b n) -> p b n", n=WIN)

        def wide_psum(b):
            return psum[:, b // 4, (b % 4) * WIDE:(b % 4 + 1) * WIDE]

        count_stage = norm_t[:, 0:KEYS].bitcast(F16).rearrange("p (s h n) -> p s h n", s=2, n=WIN)
        assert KEYS <= T

        def adj_psum(j):
            return psum[:, 6 + j % 2, 0:KEYS]

        const_ready = sem("const_ready")
        src_in = sem("src_in")
        rows_in = sem("rows_in")
        norm_in = sem("norm_in")
        comp_zeroed = sem("comp_zeroed")
        comp_in = sem("comp_in")
        weights_in = sem("weights_in")
        prep = sem("prep")
        srcf_ready = sem("srcf_ready")
        cols_ready = sem("cols_ready")
        rows_ready = sem("rows_ready")
        comp_split = sem("comp_split")
        src_turned = sem("src_turned")
        cols_turned = sem("cols_turned")
        turned = sem("turned")
        norm_turned = sem("norm_turned")
        src_t_ready = sem("src_t_ready")
        flag_ready = sem("flag_ready")
        etype_rows_in = sem("etype_rows_in")
        etype16_ready = sem("etype16_ready")
        relations_out = sem("relations_out")
        etype_in = [sem(f"etype_in{i}") for i in range(4)]
        hot_built = sem("hot_built")
        coef_mm = sem("coef_mm")
        coef_ready = sem("coef_ready")
        zeroed = sem("zeroed")
        slots_ready = sem("slots_ready")
        gather_in = [sem(f"gather_in{i}") for i in range(RING)]
        attrs_in = [sem(f"attrs_in{i}") for i in range(2)]
        hot_ready = sem("hot_ready")
        select_ready = sem("select_ready")
        tile_mm = sem("tile_mm")
        sums_mm = sem("sums_mm")
        added = sem("added")
        key_ready = sem("key_ready")
        adj_zeroed = sem("adj_zeroed")
        adj_copied = sem("adj_copied")
        adj_added = sem("adj_added")
        adj_out = [sem(f"adj_out{i}") for i in range(RING)]
        table_ready = sem("table_ready")
        ident_ready = sem("ident_ready")
        parts_step = sem("parts_step")
        parts_ready = sem("parts_ready")
        adj_in = [sem(f"adj_in{i}") for i in range(2)]
        nbr_mm = sem("nbr_mm")
        nbr_added = sem("nbr_added")
        round_done = [sem(f"round_done{r}") for r in range(2)]
        wide_slot = [sem(f"wide_slot{r}") for r in range(2)]
        wide_gather = [sem(f"wide_gather{r}") for r in range(2)]
        wide_attr = sem("wide_attr")
        wide_hot = [sem(f"wide_hot{r}") for r in range(2)]
        wide_select = sem("wide_select")
        wide_mm = [sem(f"wide_mm{r}") for r in range(2)]
        wide_add = [sem(f"wide_add{r}") for r in range(2)]
        wide_tile = [sem(f"wide_tile{r}") for r in range(2)]
        x_in = [sem(f"x_in{i}") for i in range(2)]
        agg_mm = sem("agg_mm")
        agg_relu = sem("agg_relu")
        agg_turned = sem("agg_turned")
        res_ready = [sem(f"res_ready{r}") for r in range(2)]
        ln_stats = [sem(f"ln_stats{r}") for r in range(2)]
        ln_var = [sem(f"ln_var{r}") for r in range(2)]
        ln_std_ready = [sem(f"ln_std_ready{r}") for r in range(2)]
        ln_rstd_ready = [sem(f"ln_rstd_ready{r}") for r in range(2)]
        x1_ready = sem("x1_ready")
        x1_out = [sem(f"x1_out{i}") for i in range(2)]
        x1_turned = sem("x1_turned")
        x1_t_ready = sem("x1_t_ready")
        rst_ready = sem("rst_ready")
        hidden_mm = sem("hidden_mm")
        hidden_ready = sem("hidden_ready")
        bn_step = sem("bn_step")
        bn_var = sem("bn_var")
        bn_std_ready = sem("bn_std_ready")
        bn_ready = sem("bn_ready")
        relu_ready = sem("relu_ready")
        out_mm = sem("out_mm")
        out_t_ready = sem("out_t_ready")
        out_turned = sem("out_turned")
        out_ready = sem("out_ready")
        out_done = sem("out_done")

        passed = sem("passed")

        block = ctx.enter_context(nc.Block())

        def wait_alone(engine, semaphore, value):
            engine.wait_ge(semaphore, value)
            engine.sem_inc(passed, 1)

        def read_flag(engine, which):
            engine.wait_ge(flag_ready, 1)
            return nc.values_load(wide_flag[0:1, 0:1], engines=(which,), min_val=0, max_val=1,
                                  skip_runtime_bounds_check_because="a comparison's result")

        def chunk_pipeline(engine, *stages):
            def step(k, s):
                for lag, stage in enumerate(stages):
                    if isinstance(k, int) and not 0 <= k - lag <= CHUNKS:
                        continue
                    rest = isinstance(k, int) and k - lag == CHUNKS
                    stage(k - lag, (s - lag) % 2, REST if rest else CHUNK)
            assert len(stages) <= 3
            step(0, 0)
            step(1, 1)
            with engine.Fori(1, CHUNKS // 2) as i:
                for s in range(2):
                    step(i * 2 + s, s)
            for k in range(CHUNKS, CHUNKS + len(stages)):
                step(k, k % 2)

        def tiles_of(n):
            return [(i, min(P, n - i * P)) for i in range(-(-n // P))]

        def span(k, n):
            return bass.ds(k * CHUNK, n)

        attr_tiles = edge_attr[0:(T - 1) * P, :].rearrange("(t p) f -> p t f", p=P)
        last_edges = slice(E - P, E)

        @block.sync
        def _(sp):
            def load_rows(rows, ap, signal):
                sp.dma_start(rows[:, 0:3, :],
                             ap[0:3 * TQ * P].rearrange("(q t e) -> t q e", t=TQ, e=P)).then_inc(signal, 16)
                sp.dma_start(rows[0:TQ - 1, 3, :],
                             ap[3 * TQ * P:(T - 1) * P].rearrange("(t e) -> t e", e=P)).then_inc(signal, 16)
                sp.dma_start(rows[TQ - 1:TQ, 3, :],
                             ap[last_edges].rearrange("(t e) -> t e", e=P)).then_inc(signal, 16)

            load_rows(src_rows, src, src_in)
            load_rows(etype_rows, etype, etype_rows_in)
            sp.wait_ge(ident_ready, 1)
            full = (HIGHS - 1) * P
            sp.dma_start(x_table[0:full, F:ROW].rearrange("(h p) f -> p h f", p=P),
                         ident16[:, :].bitcast(F32).unsqueeze(1).to_broadcast([P, HIGHS - 1, P // 2])
                         ).then_inc(table_ready, 16)
            sp.dma_start(x_table[full:N, F:ROW], ident16[0:N - full, :].bitcast(F32)).then_inc(table_ready, 16)
            load_rows(dst_rows, dst, rows_in)
            sp.wait_ge(etype16_ready, 1)
            sp.dma_start(relations.rearrange("q t e -> t q e"), etype16_rows[:, :, :]).then_inc(relations_out, 16)
            load_rows(norm_rows, norm, norm_in)

            sp.wait_ge(relations_out, 16)
            with sp.Fori(0, PIECES // 4) as i:
                for s in range(4):
                    wait_alone(sp, hot_built, i * 4 + s + 1)
                    for q in range(4):
                        sp.dma_start(etype_bc[32 * q:32 * q + 32, s, :],
                                     relations[q, bass.ds((i * 4 + s) * PQ, PQ), :].rearrange("t e -> (t e)")
                                     .partition_broadcast(32)).then_inc(etype_in[s], 16)

            wide = read_flag(sp, ENGINE.SP)
            with sp.If(wide < 1):
                def load_attrs(g, s, last, first=False):
                    if not first:
                        wait_alone(sp, sums_mm, g - 1)
                    lo = s % 2 * GROUP
                    sp.dma_start(attrs[:, lo:lo + GROUP - 1, :],
                                 attr_tiles[:, bass.ds(g * GROUP, GROUP - 1), :]).then_inc(attrs_in[s % 2], 16)
                    sp.dma_start(attrs[:, lo + GROUP - 1, :],
                                 edge_attr[last_edges, :] if last else
                                 edge_attr[bass.ds((g * GROUP + GROUP - 1) * P, P), :]).then_inc(attrs_in[s % 2], 16)

                def store_adjacency(g, s):
                    wait_alone(sp, adj_added, g * GROUP + GROUP + 2)
                    sp.dma_start(adjacency[:, bass.ds(g, 1), :].rearrange("p g n -> p (g n)"),
                                 adj_ring[:, s, :]).then_inc(adj_out[s], 16)

                load_attrs(0, 0, False, first=True)
                load_attrs(1, 1, False, first=True)
                with sp.Fori(0, GROUPS // RING - 1) as i:
                    for s in range(RING):
                        load_attrs(i * RING + s + 2, s, False)
                        store_adjacency(i * RING + s, s)
                for s in range(RING):
                    g = GROUPS - RING + s
                    if g + 2 < GROUPS:
                        load_attrs(g + 2, s, g + 3 == GROUPS)
                    store_adjacency(g, s)
                for s in range(RING):
                    sp.wait_ge(adj_out[s], 16 * (GROUPS // RING))

                def load_block(b, s):
                    wait_alone(sp, nbr_mm, b + 1)
                    sp.dma_start(adj_blocks[s].rearrange("p g h n -> p (g h n)"),
                                 adjacency[:, bass.ds(b * BLOCK, BLOCK), :].rearrange("p g n -> p (g n)")
                                 ).then_inc(adj_in[s], 16)
                load_block(0, 0)
            with sp.Else():
                def load_attr(t, rows):
                    wait_alone(sp, wide_tile[0], t + 1)
                    sp.dma_start(attrs[:, 0, :], rows).then_inc(wide_attr, 16)

                with sp.Fori(0, T - 1) as t:
                    load_attr(t, edge_attr[bass.ds(t * P, P), :])
                load_attr(T - 1, edge_attr[last_edges, :])

            sp.wait_ge(round_done[0], 1)

            def rows_of(table, k, n):
                if n == CHUNK:
                    return table[bass.ds(k * CHUNK, CHUNK), :].rearrange("(t p) f -> p t f", p=P)
                return table[k * CHUNK:k * CHUNK + n, :]

            def stage_rows(s, n):
                return node_stage[:, s, :, :] if n == CHUNK else node_stage[0:n, s, 0, :]

            def load_x(k, s, n):
                sp.dma_start(stage_rows(s, n), rows_of(x, k, n)).then_inc(x_in[s], 16)

            def store_x1(i, k, s, n):
                wait_alone(sp, x1_ready, (k + 2) * CT + len(tiles_of(n)))
                sp.dma_start(rows_of(x1_table, k, n), stage_rows(s, n)).then_inc(x1_out[s], 16)

            def reload(i, k, s, n):
                wait_alone(sp, x1_out[s], i * 16 + 16)
                wait_alone(sp, x1_turned, k - 1)
                wait_alone(sp, parts_ready, k - 1)
                load_x(k, s, n)

            load_x(0, 0, CHUNK)
            load_x(1, 1, CHUNK)
            with sp.Fori(0, CHUNKS // 2 - 1) as i:
                for s in range(2):
                    store_x1(i, i * 2 + s, s, CHUNK)
                    reload(i, i * 2 + s + 2, s, CHUNK)
            store_x1(CHUNKS // 2 - 1, CHUNKS - 2, 0, CHUNK)
            reload(CHUNKS // 2 - 1, CHUNKS, 0, REST)
            store_x1(CHUNKS // 2 - 1, CHUNKS - 1, 1, CHUNK)
            store_x1(CHUNKS // 2, CHUNKS, 0, REST)
            sp.wait_ge(x1_out[0], 16 * (CHUNKS // 2 + 1))
            sp.wait_ge(x1_out[1], 16 * (CHUNKS // 2))

            sp.wait_ge(agg_mm, CHUNKS + 1)
            with sp.If(wide < 1):
                load_block(1, 1)
                with sp.Fori(1, BLOCKS // 2) as i:
                    for s in range(2):
                        load_block(i * 2 + s, s)
                load_block(BLOCKS - 1, 0)

            def store_out(k, s, n):
                wait_alone(sp, out_ready, (k + 2) * CT + len(tiles_of(n)))
                sp.dma_start(rows_of(out, k, n), out_stage[:, bass.ds(k * CT, CT), :] if n == CHUNK
                             else out_stage[0:n, k * CT, :]).then_inc(out_done, 16)

            chunk_pipeline(sp, store_out)
            sp.wait_ge(out_done, 16 * (CHUNKS + 1))

        @block.gpsimd
        def _(pool):
            nc.gpsimd.memset(ident[:, :], 0.0).then_inc(const_ready, 1)
            nc.gpsimd.memset(comp_diag[:, :, :], 0.0).then_inc(comp_zeroed, 1)
            pool.wait_ge(const_ready, 1)
            nc.gpsimd.affine_select(out=ident[:, :], in_=ident[:, :], compare_op=ALU.not_equal, fill=1.0,
                                    base=0, pattern=[[-1, P]], channel_multiplier=1).then_inc(const_ready, 1)
            IMPRECISE = dict(allow_small_or_imprecise_dtypes=True)
            nc.gpsimd.iota(iota_win[:, :], [[1, WIN]], base=0, channel_multiplier=0, **IMPRECISE).then_inc(const_ready, 1)
            nc.gpsimd.iota(iota_wide[:, :], [[1, WIDE]], base=0, channel_multiplier=0, **IMPRECISE).then_inc(const_ready, 1)
            nc.gpsimd.iota(wide_starts[:, :], [[WIDE, WIDES]], base=0, channel_multiplier=0, **IMPRECISE).then_inc(const_ready, 1)
            nc.gpsimd.iota(iota_col[:, :], [[1, 1]], base=0, channel_multiplier=1, **IMPRECISE).then_inc(const_ready, 1)
            for q in range(4):
                pool.wait_ge(const_ready, 6 + q)
                nc.gpsimd.iota(relation_col[32 * q:32 * q + 32, :], [[1, 1]], base=0, channel_multiplier=1,
                               **IMPRECISE).then_inc(const_ready, 1)
            pool.wait_ge(const_ready, 10)
            nc.gpsimd.iota(iota_key[:, :], [[1, KEYS]], base=0, channel_multiplier=0, **IMPRECISE).then_inc(const_ready, 1)
            nc.gpsimd.memset(zero_col[:, :], 0.0).then_inc(const_ready, 1)
            nc.gpsimd.memset(ln_eps_col[:, :], LN_EPS).then_inc(const_ready, 1)

            def gather_group(g, s):
                wait_alone(pool, slots_ready, g + 1)
                for j in range(s * GROUP, (s + 1) * GROUP):
                    pool.indirect_dma_start(
                        gathered[:, j, :], None, x_table[:, :],
                        bass.IndirectOffsetOnAxis(src_slots[:, j:j + 1], 0)).then_inc(gather_in[s], 16)

            pool.wait_ge(table_ready, 48)
            for s in range(RING):
                gather_group(s, s)
            wide = read_flag(pool, ENGINE.Pool)
            with pool.If(wide < 1):
                with pool.Fori(1, GROUPS // RING) as i:
                    for s in range(RING):
                        gather_group(i * RING + s, s)
            with pool.Else():
                for s in range(RING):
                    pool.wait_ge(gather_in[s], 16 * GROUP)
                for r, table in enumerate((x_table, x1_table)):
                    if r == 1:
                        pool.wait_ge(x1_out[0], 16 * (CHUNKS // 2 + 1))
                        pool.wait_ge(x1_out[1], 16 * (CHUNKS // 2))
                        pool.wait_ge(parts_ready, CHUNKS + 1)
                    with pool.Fori(0, T) as t:
                        wait_alone(pool, wide_slot[r], t + 1)
                        pool.indirect_dma_start(
                            gathered[:, 0, 0:table.shape[1]], None, table[:, :],
                            bass.IndirectOffsetOnAxis(src_slots[:, 0:1], 0)).then_inc(wide_gather[r], 16)

        @block.scalar
        def _(act):
            act.sem_inc(agg_relu, 2)
            act.sem_inc(x1_t_ready, 2)
            act.sem_inc(hidden_ready, 4)
            act.dma_start(x_table[:, 0:F], x[:, :]).then_inc(table_ready, 16)
            act.wait_ge(comp_zeroed, 1)
            for q in range(4):
                act.dma_start(comp_diag[32 * q:32 * q + 32, q, :], w_comp[:, :]).then_inc(comp_in, 16)
            act.wait_ge(const_ready, 2)
            nc.scalar.activation(ident16[:, :], ident[:, :], ACT.Copy).then_inc(ident_ready, 1)
            def copy_slots(g, s):
                act.wait_ge(tile_mm, g * GROUP + GROUP)
                nc.scalar.activation(src_slots[:, s * GROUP:(s + 1) * GROUP],
                                     src_t[:, bass.ds(g * GROUP, GROUP)], ACT.Copy).then_inc(slots_ready, 1)

            act.wait_ge(src_t_ready, 1)
            for s in range(RING):
                copy_slots(s, s)
            act.dma_start(bias0_col[:, :], bias0.rearrange("(p a) -> p a", a=1)).then_inc(weights_in, 16)
            act.dma_start(b2_col[:, :], b2.rearrange("(p a) -> p a", a=1)).then_inc(weights_in, 16)
            for col, vec in ((b1_col, b1), (gamma_col, gamma), (beta_col, beta)):
                for j in range(2):
                    act.dma_start(col[:, j:j + 1],
                                  vec[j * P:(j + 1) * P].rearrange("(p a) -> p a", a=1)).then_inc(weights_in, 16)
            act.dma_start(eps_col[:, :], eps.partition_broadcast(P)).then_inc(weights_in, 16)
            act.wait_ge(const_ready, 13)
            nc.scalar.activation(sums_flat[:, :], zero_col[:, 0:1].to_broadcast([P, (B + 1) * NP + SPREAD]),
                                 ACT.Copy).then_inc(zeroed, 1)

            wide = read_flag(act, ENGINE.Activation)

            def zero_adjacency(s, j):
                size = HIGHS * SPREAD // GROUP
                nc.scalar.activation(adj_ring[:, s, j * size:(j + 1) * size], zero_col[:, 0:1].to_broadcast([P, size]),
                                     ACT.Copy).then_inc(adj_zeroed, 1)

            def count_step(i, s, zeroes, slots):
                g = i * RING + s
                if zeroes and not (isinstance(i, int) and g < 2):
                    act.wait_ge(adj_out[(s + 2) % RING], i * 16 + (16 if s >= 2 else 0))
                for j in range(GROUP):
                    act.wait_ge(tile_mm, (g + RING) * GROUP + j + 1)
                    act.wait_ge(adj_added, g * GROUP + j + 1)
                    nc.scalar.activation(count_stage[:, j % 2, :, :], adj_psum(j).rearrange("p (h n) -> p h n", n=WIN),
                                         ACT.Copy).then_inc(adj_copied, 1)
                    if zeroes:
                        zero_adjacency((s + 2) % RING, j)
                if slots:
                    copy_slots(g + RING, s)

            with act.If(wide < 1):
                act.sem_inc(adj_copied, 2)
                act.wait_ge(coef_ready, PIECES + 2)
                for s in range(2):
                    for j in range(GROUP):
                        zero_adjacency(s, j)
                for s in range(RING):
                    count_step(0, s, True, True)
                with act.Fori(1, GROUPS // RING - 1) as i:
                    for s in range(RING):
                        count_step(i, s, True, True)
                for s in range(RING):
                    count_step(GROUPS // RING - 1, s, s < 2, False)

            def wide_slots(r):
                with act.If(wide > 0):
                    for s in range(RING):
                        act.wait_ge(gather_in[s], 16 * GROUP)
                    with act.Fori(0, T) as t:
                        act.wait_ge(wide_tile[r], t + 1)
                        nc.scalar.activation(src_slots[:, 0:1], src_t[:, bass.ds(t, 1)], ACT.Copy).then_inc(wide_slot[r], 1)

            wide_slots(0)
            act.wait_ge(round_done[0], 1)
            act.dma_start(w_base, weight.rearrange("b i o -> i b o")).then_inc(weights_in, 16)
            act.dma_start(w1_sb, w1[:, :]).then_inc(weights_in, 16)
            act.dma_start(w2_sb, w2.rearrange("(j p) o -> p j o", p=P)).then_inc(weights_in, 16)

            def relu_agg(k, s, n):
                act.wait_ge(agg_mm, k + 1)
                act.wait_ge(agg_turned, k + 1)
                nc.scalar.activation(layer_stage[:, s, 0:n], psum[:, s, 0:n], ACT.Relu,
                                     bias=bias0_col[:, 0:1]).then_inc(agg_relu, 1)

            def deviations(r):
                def stage(k, s, n):
                    c, rows = len(tiles_of(n)), min(n, P)
                    act.wait_ge(ln_var[r], k * CT + c)
                    nc.scalar.activation(ln_std[0:rows, s, 0:c], ln_mv[0:rows, s, 0:c, 1], ACT.Sqrt,
                                         bias=ln_eps_col[0:rows, 0:1]).then_inc(ln_std_ready[r], 1)
                return stage

            def keep_x1(k, s, n):
                act.wait_ge(x1_turned, k + 1)
                nc.scalar.activation(x1_t[:, span(k, n)], psum[:, 4 + s, 0:n], ACT.Copy).then_inc(x1_t_ready, 1)

            act.wait_ge(weights_in, 16 * 12)
            chunk_pipeline(act, relu_agg, deviations(0), keep_x1)

            wide_slots(1)

            def keep_hidden(k, s, n):
                act.wait_ge(hidden_mm, k + 1)
                for j in range(2):
                    nc.scalar.activation(hidden[:, j, span(k, n)], psum[:, 2 * s + j, 0:n], ACT.Identity,
                                         bias=b1_col[:, j:j + 1]).then_inc(hidden_ready, 1)

            chunk_pipeline(act, keep_hidden)
            act.wait_ge(bn_var, 2)
            nc.scalar.activation(bn_std[:, :], bn_mv[:, :, 1], ACT.Sqrt, bias=ln_eps_col[:, 0:1]).then_inc(bn_std_ready, 1)
            act.wait_ge(bn_ready, 1)

            def relu_hidden(k, s, n):
                act.wait_ge(out_mm, k + 1)
                for j in range(2):
                    nc.scalar.activation(relu_stage[:, s, j, 0:n], hidden[:, j, span(k, n)], ACT.Relu,
                                         bias=bn_shift[:, j:j + 1], scale=bn_scale[:, j:j + 1]).then_inc(relu_ready, 1)

            chunk_pipeline(act, relu_hidden, deviations(1))

        @block.tensor
        def _(pe):
            pe.sem_inc(coef_mm, 4)
            pe.sem_inc(tile_mm, RING * GROUP)
            pe.sem_inc(nbr_mm, 2)
            pe.sem_inc(agg_turned, 2)
            pe.sem_inc(out_mm, 2)
            pe.sem_inc(out_turned, 2)

            def turn(rows, bank):
                for q in range(4):
                    last = nc.tensor.transpose(psum[:, bank, q * TQ:(q + 1) * TQ], rows[:, q, :], ident[0:TQ, 0:TQ])
                return last

            pe.wait_ge(const_ready, 2)
            pe.wait_ge(srcf_ready, 1)
            turn(srcf_rows, 0).then_inc(src_turned, 1)
            pe.wait_ge(cols_ready, 1)
            for bank, col in ((4, base_col), (5, span_col)):
                for q in range(4):
                    last = nc.tensor.matmul(psum[0:1, bank, q * TQ:(q + 1) * TQ], col[:, q:q + 1],
                                            ident[0:TQ, 0:TQ], start=True, stop=True)
            last.then_inc(cols_turned, 1)
            pe.wait_ge(rows_ready, 1)
            turn(rel_rows, 1)
            turn(dstf_rows, 2)
            turn(key_rows, 3).then_inc(turned, 1)

            def coefficient_products(m, s):
                pe.wait_ge(hot_built, m + 5)
                pe.wait_ge(coef_ready, m + 1)
                for j in range(PQ):
                    for part in range(3):
                        last = nc.tensor.matmul(psum[:, 6 + s % 2, j * 4 * B:(j + 1) * 4 * B],
                                                etype_hot[:, s, j * P:(j + 1) * P], comp_parts[:, part, :],
                                                start=(part == 0), stop=(part == 2))
                last.then_inc(coef_mm, 1)

            pe.wait_ge(norm_in, 16 * 3)
            turn(norm_rows, 0).then_inc(norm_turned, 1)
            pe.wait_ge(comp_split, 1)
            with pe.Fori(0, PIECES // 4) as i:
                for s in range(4):
                    coefficient_products(i * 4 + s, s)

            wide = read_flag(pe, ENGINE.PE)

            def narrow_sums():
                pe.wait_ge(coef_ready, PIECES + 2)
                def sums_start(i, s):
                    g = i * RING + s
                    turns, s = (i, s) if s < RING else (i + 1, 0)
                    pe.wait_ge(gather_in[s], turns * 16 * GROUP + 16 * GROUP)
                    pe.wait_ge(attrs_in[s % 2], turns * 64 + s // 2 * 32 + 32)
                    pe.wait_ge(select_ready, g + 1)
                    pe.wait_ge(added, g * GROUP + GROUP + 1)

                def sums_of_tile(s, j):
                    s = s % RING
                    ps = tile_psum(s % 2, j)
                    nc.tensor.matmul(ps[:, 0:B, :], gathered[:, s * GROUP + j, 0:F], weighted[:, s % 2, j, :, :],
                                     start=True, stop=True)
                    last = nc.tensor.matmul(ps[:, B, :], attrs[:, s % 2 * GROUP + j, :], hot[:, s % 2, j, :],
                                            start=True, stop=True)
                    if j == GROUP - 1:
                        last.then_inc(sums_mm, 1)

                def step(i, s, more):
                    g = i * RING + s
                    if more:
                        sums_start(i, s + 1)
                    for j in range(GROUP):
                        if more:
                            sums_of_tile(s + 1, j)
                        pe.wait_ge(key_ready, g * GROUP + j + 1)
                        pe.wait_ge(adj_copied, g * GROUP + j + 1)
                        nc.tensor.matmul(adj_psum(j), gathered[:, s * GROUP + j, F:ROW].bitcast(F16),
                                         key_hot[:, s % 2, j, :], start=True, stop=True).then_inc(tile_mm, 1)

                sums_start(0, 0)
                for j in range(GROUP):
                    sums_of_tile(0, j)
                with pe.Fori(0, GROUPS // RING - 1) as i:
                    for s in range(RING):
                        step(i, s, True)
                for s in range(RING):
                    step(GROUPS // RING - 1, s, s < RING - 1)

            def neighbours():
                pe.wait_ge(parts_ready, CHUNKS + 1)

                def block_sums(i, b, s):
                    pe.wait_ge(adj_in[s], i * 16 + 16)
                    pe.wait_ge(nbr_added, b * BLOCK + BLOCK + 1)
                    for h in range(HIGHS):
                        for c in range(3):
                            last = nc.tensor.matmul(psum[:, s, 0:BLOCK * SPREAD], x1_parts[:, h, c, :],
                                                    adj_blocks[s][:, :, h, :], start=(h + c == 0),
                                                    stop=(h == HIGHS - 1 and c == 2))
                    last.then_inc(nbr_mm, 1)

                with pe.Fori(0, BLOCKS // 2) as i:
                    for s in range(2):
                        block_sums(i, i * 2 + s, s)
                block_sums(BLOCKS // 2, BLOCKS - 1, 0)

            def edge_round(r):
                with pe.If(wide < 1):
                    if r == 0:
                        narrow_sums()
                    else:
                        neighbours()
                with pe.Else():
                    with pe.Fori(0, T) as t:
                        wait_alone(pe, wide_gather[r], t * 16 + 16)
                        if r == 0:
                            wait_alone(pe, wide_attr, t * 16 + 16)
                        with pe.Fori(0, WIDES) as w:
                            if r == 0:
                                pe.wait_ge(wide_select, t * WIDES + w + 1)
                                for h in range(B // 4):
                                    nc.tensor.matmul(psum[:, h, 0:4 * WIDE], gathered[:, 0, 0:F],
                                                     wide_weighted[:, 4 * h:4 * h + 4, :], start=True, stop=True)
                                last = nc.tensor.matmul(wide_psum(B), attrs[:, 0, :], wide_hot_sb[:, :],
                                                        start=True, stop=True)
                            else:
                                pe.wait_ge(wide_hot[r], t * WIDES + w + 1)
                                last = nc.tensor.matmul(wide_psum(B), gathered[:, 0, 0:F], wide_hot_sb[:, :],
                                                        start=True, stop=True)
                            last.then_inc(wide_mm[r], 1)

            edge_round(0)
            pe.wait_ge(round_done[0], 1)

            def turn_chunk(bank, source, n, tiles_in):
                for i, rows in tiles_of(n):
                    if tiles_in == "feature":
                        last = nc.tensor.transpose(psum[0:rows, bank, i * P:(i + 1) * P],
                                                   source[:, i * P:i * P + rows], ident[:, :])
                    else:
                        last = nc.tensor.transpose(psum[:, bank, i * P:i * P + rows],
                                                   source[0:rows, i, :], ident[0:rows, 0:rows])
                return last

            def through_bases(k, s, n):
                pe.wait_ge(agg_relu, k + 1)
                for b in range(B):
                    last = nc.tensor.matmul(psum[:, s, 0:n], w_base[:, b, :], sums[:, b, span(k, n)],
                                            start=(b == 0), stop=(b == B - 1))
                last.then_inc(agg_mm, 1)

            def turn_agg(k, s, n):
                pe.wait_ge(agg_relu, k + 3)
                pe.wait_ge(x1_ready, k * CT + CT)
                turn_chunk(2 + s, layer_stage[:, s, :], n, "feature").then_inc(agg_turned, 1)

            def turn_x1(k, s, n):
                pe.wait_ge(x1_ready, (k + 2) * CT + len(tiles_of(n)))
                pe.wait_ge(x1_t_ready, k + 1)
                turn_chunk(4 + s, node_stage[:, s, :, :], n, "node").then_inc(x1_turned, 1)

            pe.wait_ge(weights_in, 16 * 12)
            chunk_pipeline(pe, through_bases, turn_agg, turn_x1)

            pe.wait_ge(x1_t_ready, CHUNKS + 3)
            edge_round(1)

            def into_hidden(k, s, n):
                pe.wait_ge(rst_ready, k + 1)
                pe.wait_ge(hidden_ready, k * 2 + 2)
                for j in range(2):
                    last = nc.tensor.matmul(psum[:, 2 * s + j, 0:n], w1_sb[:, j * P:(j + 1) * P],
                                            sums[:, B, span(k, n)], start=True, stop=True)
                last.then_inc(hidden_mm, 1)

            chunk_pipeline(pe, into_hidden)
            pe.wait_ge(bn_ready, 1)

            def into_out(k, s, n):
                pe.wait_ge(relu_ready, k * 2 + 2)
                pe.wait_ge(out_t_ready, k + 1)
                for j in range(2):
                    last = nc.tensor.matmul(psum[:, s, 0:n], w2_sb[:, j, :], relu_stage[:, s, j, 0:n],
                                            start=(j == 0), stop=(j == 1))
                last.then_inc(out_mm, 1)

            def turn_out(k, s, n):
                pe.wait_ge(out_t_ready, k + 3)
                pe.wait_ge(out_ready, k * CT + CT)
                turn_chunk(2 + s, layer_stage[:, s, :], n, "feature").then_inc(out_turned, 1)

            chunk_pipeline(pe, into_out, turn_out)

        @block.vector
        def _(dve):
            steps = [0]

            def link(instruction):
                steps[0] += 1
                instruction.then_inc(prep, 1)
                dve.wait_ge(prep, steps[0])

            dve.sem_inc(hot_built, 4)
            dve.sem_inc(coef_ready, 2)
            dve.sem_inc(added, 2 * GROUP + 1)
            dve.sem_inc(adj_added, 2)
            dve.sem_inc(nbr_added, 2 * BLOCK + 1)
            dve.sem_inc(wide_add[0], 1)
            dve.sem_inc(wide_add[1], 1)
            dve.sem_inc(wide_tile[0], 1)
            dve.sem_inc(x1_ready, 2 * CT)
            dve.sem_inc(out_t_ready, 2)
            dve.sem_inc(out_ready, 2 * CT)

            dve.wait_ge(src_in, 16 * 3)
            nc.vector.tensor_copy(srcf_rows[:, :, :], src_rows[:, :, :]).then_inc(srcf_ready, 1)
            comp, comp_rest = (c[:, :, :].rearrange("p q b -> p (q b)") for c in (comp_diag, comp_left))
            dve.wait_ge(comp_in, 64)
            link(nc.vector.tensor_scalar(comp_parts[:, 0, :], comp, 1.0, None, ALU.mult))
            link(nc.vector.tensor_tensor(comp_rest, comp, comp_parts[:, 0, :], ALU.subtract))
            link(nc.vector.tensor_scalar(comp_parts[:, 1, :], comp_rest, 1.0, None, ALU.mult))
            nc.vector.tensor_tensor(comp_parts[:, 2, :], comp_rest, comp_parts[:, 1, :], ALU.subtract).then_inc(comp_split, 1)
            dve.wait_ge(src_turned, 1)
            nc.vector.tensor_copy(src_t[:, :], psum[:, 0, 0:T]).then_inc(src_t_ready, 1)
            dve.wait_ge(etype_rows_in, 16 * 3)
            nc.vector.tensor_copy(etype16_rows[:, :, :], etype_rows[:, :, :]).then_inc(etype16_ready, 1)
            dve.wait_ge(rows_in, 16 * 3)
            link(nc.vector.tensor_copy(dstf_rows[:, :, :], dst_rows[:, :, :]))
            nc.vector.tensor_reduce(base_col[:, :], dstf_rows[:, :, :], AX_X, ALU.min)
            link(nc.vector.tensor_reduce(high_col[:, :], dstf_rows[:, :, :], AX_X, ALU.max))
            nc.vector.tensor_tensor(span_col[:, :], high_col[:, :], base_col[:, :], ALU.subtract).then_inc(cols_ready, 1)
            nc.vector.tensor_scalar(high_rows, src_rows, P.bit_length() - 1, None, ALU.logical_shift_right)
            link(nc.vector.tensor_tensor(rel_rows, dstf_rows[:, :, :],
                                         base_col[:, :].unsqueeze(2).to_broadcast([TQ, 4, P]), ALU.subtract))
            nc.vector.scalar_tensor_tensor(key_rows, high_rows, float(WIN), rel_rows, ALU.mult,
                                           ALU.add).then_inc(rows_ready, 1)
            dve.wait_ge(cols_turned, 1)
            base_psum = psum[0:1, 4, 0:T].rearrange("p (g j) -> p g j", j=GROUP)
            behind = base_row[:, :, GROUP:2 * GROUP]
            link(nc.vector.tensor_copy(base_row[:, :, 0:GROUP], base_psum))
            nc.vector.tensor_reduce(flags[:, 0:1], psum[0:1, 5, 0:T], AX_X, ALU.max)
            link(nc.vector.tensor_tensor(behind, base_psum, base_row[:, :, 0:1].to_broadcast([1, GROUPS, GROUP]),
                                         ALU.subtract))
            nc.vector.tensor_reduce(flags[:, 1:2], behind.rearrange("p g j -> p g j"), AX_XY, ALU.max)
            link(nc.vector.tensor_reduce(flags[:, 2:3], behind, AX_XY, ALU.min))
            nc.vector.tensor_scalar(flags[:, 4:5], flags[:, 0:1], float(WIN), None, ALU.is_ge)
            nc.vector.tensor_scalar(flags[:, 5:6], flags[:, 1:2], float(SPREAD - WIN + 1), None, ALU.is_ge)
            link(nc.vector.tensor_scalar(flags[:, 6:7], flags[:, 2:3], 0.0, None, ALU.is_lt))
            dve.wait_ge(turned, 1)
            nc.vector.tensor_reduce(wide_flag[:, :], flags[:, 4:7], AX_X, ALU.max).then_inc(flag_ready, 1)

            def columns():
                nc.vector.tensor_copy(rel_t[:, :], psum[:, 1, 0:T])
                nc.vector.tensor_copy(key_t[:, :], psum[:, 3, 0:T])
                nc.vector.tensor_copy(dst_t[:, :], psum[:, 2, 0:T])
                dve.wait_ge(const_ready, 13)
                link(nc.vector.tensor_scalar(own_col[:, :], iota_col[:, :], float(P - FRESH), None, ALU.is_ge))
                last_cols = [cols[:, T - 1:T] for cols in (rel_t, key_t, dst_t)]
                for last_col in last_cols:
                    last = nc.vector.tensor_scalar(last_col, last_col, FAR, own_col[:, 0:1], ALU.add, ALU.mult)
                link(last)
                for last_col in last_cols:
                    last = nc.vector.tensor_scalar(last_col, last_col, -FAR, None, ALU.add)
                link(last)

            coef_view = coef[:, :, :].rearrange("p (q t) b -> p t q b", q=4)
            norm_view = norm_t[:, :].rearrange("p (q t) -> p t q", q=4)

            def relation_hot(i, m, s):
                dve.wait_ge(etype_in[s], i * 64 + 64)
                dve.wait_ge(coef_mm, m + 1)
                nc.vector.tensor_scalar(etype_hot[:, s, :], etype_bc[:, s, :], relation_col[:, 0:1], None,
                                        ALU.is_equal).then_inc(hot_built, 1)

            def coefficients(m, s):
                dve.wait_ge(coef_mm, m + 5)
                nc.vector.tensor_tensor(
                    coef_view[:, bass.ds(m * PQ, PQ), :, :],
                    psum[:, 6 + s % 2, 0:PQ * 4 * B].rearrange("p (t q b) -> p t q b", q=4, b=B),
                    norm_view[:, bass.ds(m * PQ, PQ), :].unsqueeze(3).to_broadcast([P, PQ, 4, B]),
                    ALU.mult).then_inc(coef_ready, 1)

            def places_hot(g, s):
                nc.vector.tensor_tensor(
                    hot[:, s % 2, :, :], rel_t[:, bass.ds(g * GROUP, GROUP)].unsqueeze(2).to_broadcast([P, GROUP, WIN]),
                    iota_win[:, :].unsqueeze(1).to_broadcast([P, GROUP, WIN]), ALU.is_equal).then_inc(hot_ready, 1)

            columns()
            dve.wait_ge(norm_turned, 1)
            link(nc.vector.tensor_copy(norm_t[:, :], psum[:, 0, 0:T]))
            dve.wait_ge(relations_out, 16)
            for s in range(4):
                relation_hot(0, s, s)
            for g in range(2):
                places_hot(g, g)
            with dve.Fori(0, PIECES // 4 - 1) as i:
                for s in range(4):
                    coefficients(i * 4 + s, s)
                    relation_hot(i + 1, i * 4 + 4 + s, s)
            for s in range(4):
                coefficients(PIECES - 4 + s, s)
            dve.wait_ge(coef_ready, PIECES + 2)
            dve.wait_ge(zeroed, 1)

            wide = read_flag(dve, ENGINE.DVE)

            def weight_hot(g, s):
                dve.wait_ge(hot_ready, g + 1)
                nc.vector.tensor_tensor(
                    weighted[:, s % 2, :, :, :], hot[:, s % 2, :, :].unsqueeze(2).to_broadcast([P, GROUP, B, WIN]),
                    coef[:, bass.ds(g * GROUP, GROUP), :].unsqueeze(3).to_broadcast([P, GROUP, B, WIN]),
                    ALU.mult).then_inc(select_ready, 1)

            def keys_hot(g, s, j):
                nc.vector.tensor_scalar(key_hot[:, s % 2, j, :], iota_key[:, :], key_t[:, bass.ds(g * GROUP + j, 1)],
                                        None, ALU.is_equal).then_inc(key_ready, 1)

            def step(i, s, select_more, keys_more):
                g = i * RING + s

                def places(lo, most, why):
                    return nc.values_load_multi_w_load_instructions(
                        base_row[0:1, bass.ds(g, 1), lo:lo + GROUP].rearrange("p g j -> p (g j)"),
                        engines=(ENGINE.DVE,), min_val=0, max_val=most, skip_runtime_bounds_check_because=why)[1]

                bases = places(0, N - 1, "bases are node numbers")
                offsets = places(GROUP, SPREAD - WIN, "the flag says so")
                dve.wait_ge(sums_mm, g + 1)
                if select_more:
                    places_hot(g + 2, s)
                for j in range(GROUP):
                    window = sums[:, :, bass.ds(bases[j], WIN)]
                    counts = adj_ring[:, s, :].rearrange("p (h n) -> p h n", n=SPREAD)[:, :, bass.ds(offsets[j], WIN)]
                    dve.wait_ge(added, (g + 2) * GROUP + j + 1)
                    nc.vector.tensor_tensor(window, tile_psum(s % 2, j), window, ALU.add).then_inc(added, 1)
                    if keys_more:
                        keys_hot(g + 1, s + 1, j)
                    if j == 0:
                        dve.wait_ge(adj_zeroed, (g + 1) * GROUP)
                    dve.wait_ge(adj_copied, g * GROUP + j + 3)
                    dve.wait_ge(adj_added, g * GROUP + j + 2)
                    nc.vector.tensor_tensor(counts, count_stage[:, j % 2, :, :], counts, ALU.add).then_inc(adj_added, 1)
                    if select_more and j == 0:
                        weight_hot(g + 2, s)

            def narrow_sums():
                for g in range(2):
                    weight_hot(g, g)
                for j in range(GROUP):
                    keys_hot(0, 0, j)
                with dve.Fori(0, GROUPS // RING - 1) as i:
                    for s in range(RING):
                        step(i, s, True, True)
                for s in range(RING):
                    step(GROUPS // RING - 1, s, s < RING - 2, s < RING - 1)
                dve.wait_ge(added, T + 2 * GROUP + 1)

            def neighbours():
                def block(b, s):
                    firsts = nc.values_load_multi_w_load_instructions(
                        base_row[0:1, bass.ds(b * BLOCK, BLOCK), 0], engines=(ENGINE.DVE,), min_val=0,
                        max_val=N - 1, skip_runtime_bounds_check_because="bases are node numbers")[1]
                    dve.wait_ge(nbr_mm, b + 3)
                    for j in range(BLOCK):
                        window = sums_flat[:, bass.ds(firsts[j] + B * NP, SPREAD)]
                        dve.wait_ge(nbr_added, b * BLOCK + 2 * BLOCK + 1 + j)
                        nc.vector.tensor_tensor(window, psum[:, s, j * SPREAD:(j + 1) * SPREAD], window,
                                                ALU.add).then_inc(nbr_added, 1)

                with dve.Fori(0, BLOCKS // 2) as i:
                    for s in range(2):
                        block(i * 2 + s, s)
                block(BLOCKS - 1, 0)
                dve.wait_ge(nbr_added, GROUPS + 2 * BLOCK + 1)

            def edge_round(r):
                with dve.If(wide < 1):
                    if r == 0:
                        narrow_sums()
                    else:
                        neighbours()
                with dve.Else():
                    adds = 2 if r == 0 else 1
                    with dve.Fori(0, T) as t:
                        with dve.Fori(0, WIDES) as w:
                            j = t * WIDES + w
                            dve.wait_ge(wide_add[r], j * adds + 1)
                            nc.vector.tensor_scalar(wide_hot_sb[:, :], iota_wide[:, :], wide_starts[:, bass.ds(w, 1)],
                                                    dst_t[:, bass.ds(t, 1)], ALU.add, ALU.is_equal).then_inc(wide_hot[r], 1)
                            if r == 0:
                                dve.wait_ge(wide_hot[r], j + 1)
                                nc.vector.tensor_tensor(
                                    wide_weighted[:, :, :], wide_hot_sb[:, :].unsqueeze(1).to_broadcast([P, B, WIDE]),
                                    coef[:, bass.ds(t, 1), :].rearrange("p t b -> p (t b)").unsqueeze(2)
                                    .to_broadcast([P, B, WIDE]), ALU.mult).then_inc(wide_select, 1)
                            dve.wait_ge(wide_mm[r], j + 1)
                            if r == 0:
                                window = sums[:, 0:B, bass.ds(w * WIDE, WIDE)].rearrange("p (h b) n -> p h b n", b=4)
                                nc.vector.tensor_tensor(
                                    window, psum[:, 0:B // 4, 0:4 * WIDE].rearrange("p h (b n) -> p h b n", b=4),
                                    window, ALU.add).then_inc(wide_add[r], 1)
                            window = sums[:, B, bass.ds(w * WIDE, WIDE)]
                            nc.vector.tensor_tensor(window, wide_psum(B), window, ALU.add).then_inc(wide_add[r], 1)
                        dve.sem_inc(wide_tile[r], 1)
                    dve.wait_ge(wide_add[r], T * WIDES * adds + 1)
                dve.sem_inc(round_done[r], 1)

            edge_round(0)

            def statistics(r, k, s, n, source):
                for i, rows in tiles_of(n):
                    nc.vector.bn_stats(ln_part[0:rows, s, i, :], source(i, rows)).then_inc(ln_stats[r], 1)
                wait_alone(dve, ln_stats[r], k * CT + len(tiles_of(n)))
                for i, rows in tiles_of(n):
                    nc.vector.bn_aggr(ln_mv[0:rows, s, i, :], ln_part[0:rows, s, i, :]).then_inc(ln_var[r], 1)

            def normalise(r, k, s, n, source, target, signal):
                c, top = len(tiles_of(n)), min(n, P)
                dve.wait_ge(ln_std_ready[r], k + 1)
                nc.vector.reciprocal(ln_rstd[0:top, s, 0:c], ln_std[0:top, s, 0:c]).then_inc(ln_rstd_ready[r], 1)
                dve.wait_ge(ln_rstd_ready[r], k + 1)
                for i, rows in tiles_of(n):
                    nc.vector.tensor_scalar(target(i, rows), source(i, rows), ln_mv[0:rows, s, i, 0:1],
                                            ln_rstd[0:rows, s, i:i + 1], ALU.subtract, ALU.mult).then_inc(signal, 1)

            def residual(k, s, n):
                dve.wait_ge(agg_turned, k + 3)
                c, rows = len(tiles_of(n)), min(n, P)
                both = node_stage[0:rows, s, 0:c, :]
                nc.vector.tensor_tensor(both, psum[0:rows, 2 + s, 0:c * P].rearrange("p (t f) -> p t f", f=F), both,
                                        ALU.add).then_inc(res_ready[0], 1)
                dve.wait_ge(res_ready[0], k + 1)
                statistics(0, k, s, n, lambda i, rows: node_stage[0:rows, s, i, :])

            def first_residual(k, s, n):
                dve.wait_ge(x_in[s], (k - s) * 8 + 16)
                residual(k, s, n)

            def first_norm(k, s, n):
                tile = lambda i, rows: node_stage[0:rows, s, i, :]
                normalise(0, k, s, n, tile, tile, x1_ready)

            def split(k, s, n):
                c, rows = len(tiles_of(n)), min(n, P)
                x1, rest = node_stage[0:rows, s, 0:c, :], left[0:rows, s, 0:c, :]
                part = [x1_parts[0:rows, bass.ds(k * CT, c), i, :] for i in range(3)]
                dve.wait_ge(x1_ready, (k + 2) * CT + c)
                nc.vector.tensor_scalar(part[0], x1, 1.0, None, ALU.mult).then_inc(parts_step, 1)
                dve.wait_ge(parts_step, k * 3 + 1)
                nc.vector.tensor_tensor(rest, x1, part[0], ALU.subtract).then_inc(parts_step, 1)
                dve.wait_ge(parts_step, k * 3 + 2)
                nc.vector.tensor_scalar(part[1], rest, 1.0, None, ALU.mult).then_inc(parts_step, 1)
                dve.wait_ge(parts_step, k * 3 + 3)
                nc.vector.tensor_tensor(part[2], rest, part[1], ALU.subtract).then_inc(parts_ready, 1)

            link(nc.vector.memset(x1_parts[:, HIGHS - 1, :, :], 0.0))

            def norm_and_split(k, s, n):
                first_norm(k, s, n)
                split(k, s, n)

            chunk_pipeline(dve, first_residual, norm_and_split)

            dve.wait_ge(x1_ready, 2 * CT + CHUNKS * CT + 1)
            dve.sem_inc(wide_tile[1], 1)
            edge_round(1)

            link(nc.vector.tensor_scalar(one_eps[:, :], eps_col[:, :], 1.0, None, ALU.add))
            dve.wait_ge(x1_t_ready, CHUNKS + 3)

            def rst(k, s, n):
                total = sums[:, B, span(k, n)]
                nc.vector.scalar_tensor_tensor(total, x1_t[:, span(k, n)], one_eps[:, 0:1], total,
                                               ALU.mult, ALU.add).then_inc(rst_ready, 1)

            chunk_pipeline(dve, rst)

            def hidden_stats(k, s, n):
                dve.wait_ge(hidden_ready, k * 2 + 6)
                for j in range(2):
                    nc.vector.bn_stats(bn_part[:, j, bass.ds(k, 1), :].rearrange("p a c -> p (a c)"),
                                       hidden[:, j, span(k, n)]).then_inc(bn_step, 1)

            chunk_pipeline(dve, hidden_stats)
            dve.wait_ge(bn_step, 2 * (CHUNKS + 1))
            for j in range(2):
                nc.vector.bn_aggr(bn_mv[:, j, :], bn_part[:, j, :, :].rearrange("p k c -> p (k c)")).then_inc(bn_var, 1)
            dve.wait_ge(bn_std_ready, 1)
            link(nc.vector.reciprocal(bn_rstd[:, :], bn_std[:, :]))
            link(nc.vector.tensor_tensor(bn_scale[:, :], bn_rstd[:, :], gamma_col[:, :], ALU.mult))
            link(nc.vector.tensor_tensor(bn_ms[:, :], bn_mv[:, :, 0], bn_scale[:, :], ALU.mult))
            nc.vector.tensor_tensor(bn_shift[:, :], beta_col[:, :], bn_ms[:, :], ALU.subtract).then_inc(bn_ready, 1)

            def second_residual(k, s, n):
                dve.wait_ge(out_mm, k + 3)
                dve.wait_ge(out_turned, k + 1)
                nc.vector.scalar_tensor_tensor(layer_stage[:, s, 0:n], psum[:, s, 0:n], b2_col[:, 0:1],
                                               x1_t[:, span(k, n)], ALU.add, ALU.add).then_inc(out_t_ready, 1)

            def out_tile(s, i, rows):
                return psum[0:rows, 2 + s, i * P:(i + 1) * P]

            def second_stats(k, s, n):
                dve.wait_ge(out_turned, k + 3)
                statistics(1, k, s, n, lambda i, rows: out_tile(s, i, rows))

            def second_norm(k, s, n):
                normalise(1, k, s, n, lambda i, rows: out_tile(s, i, rows),
                          lambda i, rows: out_stage[0:rows, bass.ds(k * CT + i, 1), :].rearrange("p t f -> p (t f)"),
                          out_ready)

            chunk_pipeline(dve, second_residual, second_stats, second_norm)


_INS = ['x', 'src', 'dst', 'edge_attr_128', 'edge_type_32', 'edge_weight1', 'L0_gnn_weight', 'L0_gnn_w_comp',
        'L0_gnn_bias_param', 'L1_gnn_eps', 'L1_gnn_W1', 'L1_gnn_b1', 'L1_gnn_gamma', 'L1_gnn_beta', 'L1_gnn_W2',
        'L1_gnn_b2']


def kernel(**inputs):
    import numpy as _np
    import concourse.bacc as _bacc
    from concourse import mybir as _mybir
    from concourse.bass_utils import run_bass_kernel_spmd as _run

    nc = _bacc.Bacc("TRN2", target_bir_lowering=False, num_devices=1)
    arrays, args = {}, []
    for name in _INS:
        a = _np.ascontiguousarray(inputs[name])
        if name == 'edge_weight1':
            a = a.reshape(-1)
        arrays[f"in_{name}_dram"] = a
        args.append(nc.dram_tensor(f"in_{name}_dram", a.shape, _mybir.dt.from_np(a.dtype), kind="ExternalInput").ap())
    args.append(nc.dram_tensor("out_0_dram", inputs['x'].shape, _mybir.dt.float32, kind="ExternalOutput").ap())
    gnn_resnorm_kernel(nc, *args)
    r = _run(nc, [arrays], core_ids=[0])
    return r.results[0]["out_0_dram"]
```

```python
from contextlib import ExitStack

import concourse.bass as bass
from concourse import mybir

F32 = mybir.dt.float32
F16 = mybir.dt.float16
BF16 = mybir.dt.bfloat16
I32 = mybir.dt.int32
ALU = mybir.AluOpType
ACT = mybir.ActivationFunctionType
AX_X = mybir.AxisListType.X
AX_XY = mybir.AxisListType.XY
ENGINE = mybir.EngineType

P = 128
WIN = 16
GROUP = 8
RING = 4
PAIR = 2
SPREAD = 144
BLOCK = 2
CHUNK = 512
LN_EPS = 1e-5
BN_EPS = 1e-5


def gnn_resnorm_kernel(nc, x, src, dst, edge_attr, etype, norm, weight, w_comp, bias0,
                       eps, w1, b1, gamma, beta, w2, b2, out):
    N, F = x.shape
    E = src.shape[0]
    B = weight.shape[0]
    R = w_comp.shape[0]
    H = w1.shape[1]
    assert F == P and H == 2 * P and R == 32

    T = -(-E // P)
    FRESH = E - (T - 1) * P
    TQ = T // 4
    assert T == 4 * TQ and T % (GROUP * RING) == 0 and 0 < FRESH <= P
    GROUPS = T // GROUP
    NP = N + WIN - 1
    WIDE = 125
    WIDES = -(-N // WIDE)
    assert WIDES * WIDE <= NP and 4 * WIDE <= 512
    CHUNKS = N // CHUNK
    REST = N - CHUNKS * CHUNK
    CT = CHUNK // P
    assert CHUNKS % 2 == 0 and 0 < REST <= P
    PQ = 13
    PIECES = TQ // PQ
    assert TQ % PQ == 0 and PIECES == 8 and GROUP <= PQ and PQ * 4 * B <= 512 and PQ >= GROUP

    HIGHS = -(-N // P)
    KEYS = HIGHS * WIN
    FAR = 4096.0
    PAIRS = GROUPS // PAIR
    BLOCKS = PAIRS // BLOCK
    ROW = F + P // 2
    assert PAIR * GROUP * P <= 2048 and KEYS <= 512 and FAR > KEYS and BLOCKS % 2 == 1
    assert GROUPS == PAIR * PAIRS and PAIRS == BLOCK * BLOCKS and RING == PAIR * BLOCK and BLOCK * SPREAD <= 512
    assert HIGHS * SPREAD % GROUP == 0

    x_table = nc.dram_tensor("x_table", (N, ROW), F32, kind="Internal").ap()
    relations = nc.dram_tensor("relations", (4, TQ, P), F16, kind="Internal").ap()
    adjacency = nc.dram_tensor("adjacency", (P, PAIRS, HIGHS * SPREAD), F16, kind="Internal").ap()
    x1_table = nc.dram_tensor("x1_table", (N, F), F32, kind="Internal").ap()

    with ExitStack() as ctx:
        def sb(name, shape, dt=F32):
            return ctx.enter_context(nc.sbuf_tensor(name, shape, dt))

        def sem(name):
            return ctx.enter_context(nc.semaphore(name))

        attrs = sb("attrs", [P, 2 * GROUP, F])
        weighted = sb("weighted", [P, 2, GROUP, B, WIN])
        weighted_flat = weighted[:, :, :, :, :].rearrange("p s t b n -> p (s t b n)")
        rows_a = attrs[0:TQ, :, :].rearrange("p (i q) f -> p i q f", q=4)
        rows_b = weighted_flat[0:TQ, :].rearrange("p (i q f) -> p i q f", q=4, f=F)
        src_rows, high_rows, dst_rows = rows_a[:, 0].bitcast(I32), rows_a[:, 1].bitcast(I32), rows_a[:, 2].bitcast(I32)
        srcf_rows, dstf_rows, rel_rows, norm_rows, key_rows = rows_a[:, 3], rows_b[:, 0], rows_b[:, 1], rows_b[:, 2], rows_b[:, 3]
        base_col = sb("base_col", [TQ, 4])
        high_col = sb("high_col", [TQ, 4])
        span_col = sb("span_col", [TQ, 4])
        src_t = sb("src_t", [P, T])
        rel_t = sb("rel_t", [P, T])
        norm_t = sb("norm_t", [P, T])
        key_t = sb("key_t", [P, T])
        base_row = sb("base_row", [1, GROUPS, 2 * GROUP], I32)
        flags = sb("flags", [1, 8])
        wide_flag = sb("wide_flag", [1, 1], I32)
        coef = sb("coef", [P, T, B])
        coef_flat = coef[:, :, :].rearrange("p t b -> p (t b)")
        adj_flat = sb("adj_flat", [P, max(2 * HIGHS * SPREAD, 4 * PQ * P + 2 * T)], F16)
        adj_ring = adj_flat[:, 0:2 * HIGHS * SPREAD].rearrange("p (s n) -> p s n", s=2)
        assert B * WIDE <= B * F
        dst_t = adj_flat[:, 4 * PQ * P:4 * PQ * P + 2 * T].bitcast(F32)
        etype_bc = adj_flat[:, 0:4 * PQ * P].rearrange("p (s e) -> p s e", s=4)
        etype_rows = coef_flat[0:TQ, 0:4 * P].bitcast(I32).rearrange("p (q e) -> p q e", q=4)
        etype16_rows = coef_flat[0:TQ, 4 * P:6 * P].bitcast(F16).rearrange("p (q e) -> p q e", q=4)
        etype_hot_flat = sb("etype_hot", [P, 2 * PQ * P])
        etype_hot = etype_hot_flat[:, :].bitcast(BF16).rearrange("p (s e) -> p s e", s=4)
        relation_col = sb("relation_col", [P, 1])
        comp_diag = sb("comp_diag", [P, 4, B])
        comp_left = sb("comp_left", [P, 4, B])
        comp_parts = sb("comp_parts", [P, 3, 4 * B], BF16)
        ident = sb("ident", [P, P])
        ident16 = sb("ident16", [P, P], F16)
        iota_key = sb("iota_key", [P, KEYS], F16)
        iota_win = sb("iota_win", [P, WIN])
        iota_wide = sb("iota_wide", [P, WIDE])
        wide_starts = sb("wide_starts", [P, WIDES])
        iota_col = sb("iota_col", [P, 1])
        own_col = sb("own_col", [P, 1])
        zero_col = sb("zero_col", [P, 1])
        ln_eps_col = sb("ln_eps_col", [P, 1])
        WEIGHTS = 2 * CHUNK
        WEIGHTS_END = WEIGHTS + B * F + 2 * H
        assert WEIGHTS_END <= (T - RING * GROUP) * B
        w_base = coef_flat[:, WEIGHTS:WEIGHTS + B * F].rearrange("p (b o) -> p b o", b=B)
        w1_sb = coef_flat[:, WEIGHTS + B * F:WEIGHTS + B * F + H]
        w2_sb = coef_flat[:, WEIGHTS + B * F + H:WEIGHTS_END].rearrange("p (j o) -> p j o", j=2)
        bias0_col = sb("bias0_col", [P, 1])
        b1_col = sb("b1_col", [P, 2])
        gamma_col = sb("gamma_col", [P, 2])
        beta_col = sb("beta_col", [P, 2])
        b2_col = sb("b2_col", [P, 1])
        eps_col = sb("eps_col", [P, 1])
        one_eps = sb("one_eps", [P, 1])
        sums_flat = sb("sums_flat", [P, (B + 1) * NP + SPREAD])
        sums = sums_flat[:, 0:(B + 1) * NP].rearrange("p (b n) -> p b n", n=NP)
        key_hot = etype_hot_flat[:, 0:GROUP * KEYS].bitcast(F16).rearrange("p (s t n) -> p s t n", s=2, n=KEYS)
        x1_t = etype_hot_flat[:, 0:N]
        gathered = sb("gathered", [P, RING * GROUP, ROW])
        gathered_flat = gathered[:, :, :].rearrange("p t f -> p (t f)")
        src_slots = sb("src_slots", [P, RING * GROUP], I32)
        hot = sb("hot", [P, 2, GROUP, WIN])
        wide_hot_sb = weighted_flat[:, B * F + 2 * H:B * F + 2 * H + WIDE]
        wide_weighted = weighted_flat[:, 0:B * WIDE] \
            .rearrange("p (b n) -> p b n", n=WIDE)
        node_stage = attrs[:, 0:2 * CT, :].rearrange("p (s t) f -> p s t f", s=2)
        layer_stage = attrs[:, 2 * CT:4 * CT, :].rearrange("p (s t) f -> p s (t f)", s=2)
        out_stage = gathered_flat[:, 0:HIGHS * F].rearrange("p (t f) -> p t f", f=F)
        x_stage = gathered_flat[:, HIGHS * 3 * F // 2:HIGHS * 3 * F // 2 + 2 * CHUNK] \
            .rearrange("p (s t f) -> p s t f", s=2, f=F)
        x1_parts = gathered_flat[:, 0:HIGHS * 3 * F // 2].bitcast(BF16).rearrange("p (h c f) -> p h c f", c=3, f=F)
        left = coef[:, 0:2 * CHUNK // B, :].rearrange("p (s t) b -> p s (t b)", s=2).rearrange("p s (t f) -> p s t f", f=F)
        adj_blocks = [buffer.rearrange("p (g h n) -> p g h n", g=BLOCK, n=SPREAD) for buffer in
                      (adj_flat[:, 0:BLOCK * HIGHS * SPREAD], sums_flat[:, 0:BLOCK * HIGHS * SPREAD // 2].bitcast(F16))]
        hidden = sums[:, 0:2, 0:N]
        relu_stage = sums[:, 2:4, 0:2 * CHUNK].rearrange("p s (j n) -> p s j n", j=2)
        bn_part = sb("bn_part", [P, 2, CHUNKS + 1, 6])
        bn_mv = sb("bn_mv", [P, 2, 2])
        bn_std = sb("bn_std", [P, 2])
        bn_rstd = sb("bn_rstd", [P, 2])
        bn_scale = sb("bn_scale", [P, 2])
        bn_ms = sb("bn_ms", [P, 2])
        bn_shift = sb("bn_shift", [P, 2])
        ln_part = sb("ln_part", [P, 2, CT, 6])
        ln_mv = sb("ln_mv", [P, 2, CT, 2])
        ln_std = sb("ln_std", [P, 2, CT])
        ln_rstd = sb("ln_rstd", [P, 2, CT])
        ln_shift = sb("ln_shift", [P, 2, CT])

        psum = ctx.enter_context(nc.psum_tensor("psum", [P, 8, 512], F32))

        def tile_psum(slot, i):
            c = (i % 3) * (B + 1) * WIN
            return psum[:, 3 * slot + i // 3, c:c + (B + 1) * WIN].rearrange("p (b n) -> p b n", n=WIN)

        def wide_psum(b):
            return psum[:, b // 4, (b % 4) * WIDE:(b % 4 + 1) * WIDE]

        count_stage = norm_t[:, 0:KEYS].bitcast(F16).rearrange("p (s h n) -> p s h n", s=2, n=WIN)
        assert KEYS <= T

        def adj_psum(j):
            return psum[:, 6 + j % 2, 0:KEYS]

        const_ready = sem("const_ready")
        src_in = sem("src_in")
        rows_in = sem("rows_in")
        norm_in = sem("norm_in")
        comp_zeroed = sem("comp_zeroed")
        comp_in = sem("comp_in")
        weights_in = sem("weights_in")
        prep = sem("prep")
        srcf_ready = sem("srcf_ready")
        cols_ready = sem("cols_ready")
        rows_ready = sem("rows_ready")
        comp_split = sem("comp_split")
        src_turned = sem("src_turned")
        cols_turned = sem("cols_turned")
        turned = sem("turned")
        norm_turned = sem("norm_turned")
        src_t_ready = sem("src_t_ready")
        flag_ready = sem("flag_ready")
        etype_rows_in = sem("etype_rows_in")
        etype16_ready = sem("etype16_ready")
        relations_out = sem("relations_out")
        etype_in = [sem(f"etype_in{i}") for i in range(4)]
        hot_built = sem("hot_built")
        coef_mm = sem("coef_mm")
        coef_ready = sem("coef_ready")
        zeroed = sem("zeroed")
        slots_ready = sem("slots_ready")
        gather_in = [sem(f"gather_in{i}") for i in range(RING)]
        attrs_in = [sem(f"attrs_in{i}") for i in range(2)]
        hot_ready = sem("hot_ready")
        select_ready = sem("select_ready")
        tile_mm = sem("tile_mm")
        sums_mm = sem("sums_mm")
        added = sem("added")
        key_ready = sem("key_ready")
        adj_zeroed = sem("adj_zeroed")
        adj_copied = sem("adj_copied")
        adj_added = sem("adj_added")
        adj_out = [sem(f"adj_out{i}") for i in range(2)]
        table_ready = sem("table_ready")
        ident_ready = sem("ident_ready")
        parts_step = sem("parts_step")
        parts_ready = sem("parts_ready")
        adj_in = [sem(f"adj_in{i}") for i in range(2)]
        nbr_mm = sem("nbr_mm")
        nbr_added = sem("nbr_added")
        round_done = [sem(f"round_done{r}") for r in range(2)]
        wide_slot = [sem(f"wide_slot{r}") for r in range(2)]
        wide_gather = [sem(f"wide_gather{r}") for r in range(2)]
        wide_attr = sem("wide_attr")
        wide_hot = [sem(f"wide_hot{r}") for r in range(2)]
        wide_select = sem("wide_select")
        wide_mm = [sem(f"wide_mm{r}") for r in range(2)]
        wide_add = [sem(f"wide_add{r}") for r in range(2)]
        wide_tile = [sem(f"wide_tile{r}") for r in range(2)]
        x_in = [sem(f"x_in{i}") for i in range(2)]
        agg_mm = sem("agg_mm")
        agg_relu = sem("agg_relu")
        agg_turned = sem("agg_turned")
        res_ready = [sem(f"res_ready{r}") for r in range(2)]
        ln_stats = [sem(f"ln_stats{r}") for r in range(2)]
        ln_var = [sem(f"ln_var{r}") for r in range(2)]
        ln_std_ready = [sem(f"ln_std_ready{r}") for r in range(2)]
        ln_rstd_ready = [sem(f"ln_rstd_ready{r}") for r in range(2)]
        x1_ready = sem("x1_ready")
        x1_out = [sem(f"x1_out{i}") for i in range(2)]
        x1_turned = sem("x1_turned")
        x1_t_ready = sem("x1_t_ready")
        own_added = sem("own_added")
        hidden_mm = sem("hidden_mm")
        hidden_ready = sem("hidden_ready")
        bn_step = sem("bn_step")
        bn_var = sem("bn_var")
        bn_std_ready = sem("bn_std_ready")
        bn_ready = sem("bn_ready")
        relu_ready = sem("relu_ready")
        out_mm = sem("out_mm")
        out_t_ready = sem("out_t_ready")
        out_turned = sem("out_turned")
        shift_ready = sem("shift_ready")
        out_ready = sem("out_ready")
        out_done = sem("out_done")

        passed = sem("passed")

        block = ctx.enter_context(nc.Block())

        def wait_alone(engine, semaphore, value):
            engine.wait_ge(semaphore, value)
            engine.sem_inc(passed, 1)

        def read_flag(engine, which):
            engine.wait_ge(flag_ready, 1)
            return nc.values_load(wide_flag[0:1, 0:1], engines=(which,), min_val=0, max_val=1,
                                  skip_runtime_bounds_check_because="a comparison's result")

        def chunk_pipeline(engine, *stages, order=None):
            def step(k, s):
                for lag in order or range(len(stages)):
                    stage = stages[lag]
                    if stage is None or isinstance(k, int) and not 0 <= k - lag <= CHUNKS:
                        continue
                    rest = isinstance(k, int) and k - lag == CHUNKS
                    stage(k - lag, (s - lag) % 2, REST if rest else CHUNK)
            whole = 2 * (len(stages) // 2)
            whole = max(whole, 2)
            for k in range(whole):
                step(k, k % 2)
            with engine.Fori(whole // 2, CHUNKS // 2) as i:
                for s in range(2):
                    step(i * 2 + s, s)
            for k in range(CHUNKS, CHUNKS + len(stages)):
                step(k, k % 2)

        def late(k):
            return isinstance(k, int) and k >= CHUNKS - 2

        def tiles_of(n):
            return [(i, min(P, n - i * P)) for i in range(-(-n // P))]

        def span(k, n):
            return bass.ds(k * CHUNK, n)

        attr_tiles = edge_attr[0:(T - 1) * P, :].rearrange("(t p) f -> p t f", p=P)
        last_edges = slice(E - P, E)

        @block.sync
        def _(sp):
            for s in range(2):
                sp.sem_inc(x1_out[s], 16)
            def load_rows(rows, ap, signal):
                sp.dma_start(rows[:, 0:3, :],
                             ap[0:3 * TQ * P].rearrange("(q t e) -> t q e", t=TQ, e=P)).then_inc(signal, 16)
                sp.dma_start(rows[0:TQ - 1, 3, :],
                             ap[3 * TQ * P:(T - 1) * P].rearrange("(t e) -> t e", e=P)).then_inc(signal, 16)
                sp.dma_start(rows[TQ - 1:TQ, 3, :],
                             ap[last_edges].rearrange("(t e) -> t e", e=P)).then_inc(signal, 16)

            load_rows(src_rows, src, src_in)
            load_rows(etype_rows, etype, etype_rows_in)
            sp.wait_ge(ident_ready, 1)
            full = (HIGHS - 1) * P
            sp.dma_start(x_table[0:full, F:ROW].rearrange("(h p) f -> p h f", p=P),
                         ident16[:, :].bitcast(F32).unsqueeze(1).to_broadcast([P, HIGHS - 1, P // 2])
                         ).then_inc(table_ready, 16)
            sp.dma_start(x_table[full:N, F:ROW], ident16[0:N - full, :].bitcast(F32)).then_inc(table_ready, 16)
            load_rows(dst_rows, dst, rows_in)
            sp.wait_ge(etype16_ready, 1)
            sp.dma_start(relations.rearrange("q t e -> t q e"), etype16_rows[:, :, :]).then_inc(relations_out, 16)
            load_rows(norm_rows, norm, norm_in)

            sp.wait_ge(relations_out, 16)
            with sp.Fori(0, PIECES // 4) as i:
                for s in range(4):
                    wait_alone(sp, hot_built, i * 4 + s + 1)
                    for q in range(4):
                        sp.dma_start(etype_bc[32 * q:32 * q + 32, s, :],
                                     relations[q, bass.ds((i * 4 + s) * PQ, PQ), :].rearrange("t e -> (t e)")
                                     .partition_broadcast(32)).then_inc(etype_in[s], 16)

            wide = read_flag(sp, ENGINE.SP)
            with sp.If(wide < 1):
                def load_attrs(g, s, last, first=False):
                    if not first:
                        wait_alone(sp, sums_mm, g - 1)
                    lo = s % 2 * GROUP
                    sp.dma_start(attrs[:, lo:lo + GROUP - 1, :],
                                 attr_tiles[:, bass.ds(g * GROUP, GROUP - 1), :]).then_inc(attrs_in[s % 2], 16)
                    sp.dma_start(attrs[:, lo + GROUP - 1, :],
                                 edge_attr[last_edges, :] if last else
                                 edge_attr[bass.ds((g * GROUP + GROUP - 1) * P, P), :]).then_inc(attrs_in[s % 2], 16)

                def store_adjacency(i, s):
                    wait_alone(sp, adj_added, (i * RING + s) * GROUP + GROUP + 2)
                    sp.dma_start(adjacency[:, bass.ds(i * BLOCK + s // PAIR, 1), :].rearrange("p g n -> p (g n)"),
                                 adj_ring[:, s // PAIR, :]).then_inc(adj_out[s // PAIR], 16)

                load_attrs(0, 0, False, first=True)
                load_attrs(1, 1, False, first=True)
                with sp.Fori(0, GROUPS // RING - 1) as i:
                    for s in range(RING):
                        load_attrs(i * RING + s + 2, s, False)
                        if s % PAIR == PAIR - 1:
                            store_adjacency(i, s)
                for s in range(RING):
                    g = GROUPS - RING + s
                    if g + 2 < GROUPS:
                        load_attrs(g + 2, s, g + 3 == GROUPS)
                    if s % PAIR == PAIR - 1:
                        store_adjacency(GROUPS // RING - 1, s)
                for s in range(2):
                    sp.wait_ge(adj_out[s], 16 * (GROUPS // RING))

                def load_block(b, s):
                    wait_alone(sp, nbr_mm, b + 1)
                    sp.dma_start(adj_blocks[s].rearrange("p g h n -> p (g h n)"),
                                 adjacency[:, bass.ds(b * BLOCK, BLOCK), :].rearrange("p g n -> p (g n)")
                                 ).then_inc(adj_in[s], 16)
                load_block(0, 0)
            with sp.Else():
                def load_attr(t, rows):
                    wait_alone(sp, wide_tile[0], t + 1)
                    sp.dma_start(attrs[:, 0, :], rows).then_inc(wide_attr, 16)

                with sp.Fori(0, T - 1) as t:
                    load_attr(t, edge_attr[bass.ds(t * P, P), :])
                load_attr(T - 1, edge_attr[last_edges, :])

            sp.wait_ge(round_done[0], 1)

            def rows_of(table, k, n):
                if n == CHUNK:
                    return table[bass.ds(k * CHUNK, CHUNK), :].rearrange("(t p) f -> p t f", p=P)
                return table[k * CHUNK:k * CHUNK + n, :]

            def stage_rows(stage, s, n):
                return stage[:, s, :, :] if n == CHUNK else stage[0:n, s, 0, :]

            def load_x(k, s, n):
                wait_alone(sp, res_ready[0], k + 1)
                sp.dma_start(stage_rows(x_stage, s, n), rows_of(x, k, n)).then_inc(x_in[s], 16)

            def store_x1(i, k, s, n):
                wait_alone(sp, x1_ready, (k + 2) * CT + len(tiles_of(n)))
                sp.dma_start(rows_of(x1_table, k, n), stage_rows(node_stage, s, n)).then_inc(x1_out[s], 16)

            load_x(0, 0, CHUNK)
            load_x(1, 1, CHUNK)
            with sp.Fori(0, CHUNKS // 2 - 1) as i:
                for s in range(2):
                    load_x(i * 2 + s + 2, s, CHUNK)
                    store_x1(i, i * 2 + s, s, CHUNK)
            load_x(CHUNKS, 0, REST)
            with sp.If(wide < 1):
                sp.wait_ge(agg_mm, CHUNKS + 1)
                load_block(1, 1)
            for s in range(2):
                store_x1(CHUNKS // 2 - 1, CHUNKS - 2 + s, s, CHUNK)
            store_x1(CHUNKS // 2, CHUNKS, 0, REST)
            sp.wait_ge(x1_out[0], 16 * (CHUNKS // 2 + 2))
            sp.wait_ge(x1_out[1], 16 * (CHUNKS // 2 + 1))

            with sp.If(wide < 1):
                with sp.Fori(1, BLOCKS // 2) as i:
                    for s in range(2):
                        load_block(i * 2 + s, s)
                load_block(BLOCKS - 1, 0)

            def store_out(k, s, n):
                wait_alone(sp, out_ready, (k + 2) * CT + len(tiles_of(n)))
                sp.dma_start(rows_of(out, k, n), out_stage[:, bass.ds(k * CT, CT), :] if n == CHUNK
                             else out_stage[0:n, k * CT, :]).then_inc(out_done, 16)

            chunk_pipeline(sp, store_out)
            sp.wait_ge(out_done, 16 * (CHUNKS + 1))

        @block.gpsimd
        def _(pool):
            nc.gpsimd.memset(ident[:, :], 0.0).then_inc(const_ready, 1)
            nc.gpsimd.memset(comp_diag[:, :, :], 0.0).then_inc(comp_zeroed, 1)
            pool.wait_ge(const_ready, 1)
            nc.gpsimd.affine_select(out=ident[:, :], in_=ident[:, :], compare_op=ALU.not_equal, fill=1.0,
                                    base=0, pattern=[[-1, P]], channel_multiplier=1).then_inc(const_ready, 1)
            IMPRECISE = dict(allow_small_or_imprecise_dtypes=True)
            nc.gpsimd.iota(iota_win[:, :], [[1, WIN]], base=0, channel_multiplier=0, **IMPRECISE).then_inc(const_ready, 1)
            nc.gpsimd.iota(iota_wide[:, :], [[1, WIDE]], base=0, channel_multiplier=0, **IMPRECISE).then_inc(const_ready, 1)
            nc.gpsimd.iota(wide_starts[:, :], [[WIDE, WIDES]], base=0, channel_multiplier=0, **IMPRECISE).then_inc(const_ready, 1)
            nc.gpsimd.iota(iota_col[:, :], [[1, 1]], base=0, channel_multiplier=1, **IMPRECISE).then_inc(const_ready, 1)
            for q in range(4):
                pool.wait_ge(const_ready, 6 + q)
                nc.gpsimd.iota(relation_col[32 * q:32 * q + 32, :], [[1, 1]], base=0, channel_multiplier=1,
                               **IMPRECISE).then_inc(const_ready, 1)
            pool.wait_ge(const_ready, 10)
            nc.gpsimd.iota(iota_key[:, :], [[1, KEYS]], base=0, channel_multiplier=0, **IMPRECISE).then_inc(const_ready, 1)
            nc.gpsimd.memset(zero_col[:, :], 0.0).then_inc(const_ready, 1)
            nc.gpsimd.memset(ln_eps_col[:, :], LN_EPS).then_inc(const_ready, 1)

            def gather_group(g, s):
                wait_alone(pool, slots_ready, g + 1)
                for j in range(s * GROUP, (s + 1) * GROUP):
                    pool.indirect_dma_start(
                        gathered[:, j, :], None, x_table[:, :],
                        bass.IndirectOffsetOnAxis(src_slots[:, j:j + 1], 0)).then_inc(gather_in[s], 16)

            pool.wait_ge(table_ready, 48)
            for s in range(RING):
                gather_group(s, s)
            wide = read_flag(pool, ENGINE.Pool)
            with pool.If(wide < 1):
                with pool.Fori(1, GROUPS // RING) as i:
                    for s in range(RING):
                        gather_group(i * RING + s, s)
            with pool.Else():
                for s in range(RING):
                    pool.wait_ge(gather_in[s], 16 * GROUP)
                for r, table in enumerate((x_table, x1_table)):
                    if r == 1:
                        pool.wait_ge(x1_out[0], 16 * (CHUNKS // 2 + 2))
                        pool.wait_ge(x1_out[1], 16 * (CHUNKS // 2 + 1))
                        pool.wait_ge(parts_ready, CHUNKS + 1)
                    with pool.Fori(0, T) as t:
                        wait_alone(pool, wide_slot[r], t + 1)
                        pool.indirect_dma_start(
                            gathered[:, 0, 0:table.shape[1]], None, table[:, :],
                            bass.IndirectOffsetOnAxis(src_slots[:, 0:1], 0)).then_inc(wide_gather[r], 16)

        @block.scalar
        def _(act):
            act.sem_inc(agg_relu, 2)
            act.sem_inc(out_ready, 2 * CT)
            act.sem_inc(x1_t_ready, 2)
            act.sem_inc(hidden_ready, 4)
            act.dma_start(x_table[:, 0:F], x[:, :]).then_inc(table_ready, 16)
            act.wait_ge(comp_zeroed, 1)
            for q in range(4):
                act.dma_start(comp_diag[32 * q:32 * q + 32, q, :], w_comp[:, :]).then_inc(comp_in, 16)
            act.wait_ge(const_ready, 2)
            nc.scalar.activation(ident16[:, :], ident[:, :], ACT.Copy).then_inc(ident_ready, 1)
            def copy_slots(g, s):
                act.wait_ge(tile_mm, g * GROUP + GROUP)
                nc.scalar.activation(src_slots[:, s * GROUP:(s + 1) * GROUP],
                                     src_t[:, bass.ds(g * GROUP, GROUP)], ACT.Copy).then_inc(slots_ready, 1)

            act.wait_ge(src_t_ready, 1)
            for s in range(RING):
                copy_slots(s, s)
            act.wait_ge(const_ready, 13)
            nc.scalar.activation(sums_flat[:, :], zero_col[:, 0:1].to_broadcast([P, (B + 1) * NP + SPREAD]),
                                 ACT.Copy).then_inc(zeroed, 1)
            act.dma_start(bias0_col[:, :], bias0.rearrange("(p a) -> p a", a=1)).then_inc(weights_in, 16)
            act.dma_start(b2_col[:, :], b2.rearrange("(p a) -> p a", a=1)).then_inc(weights_in, 16)
            for col, vec in ((b1_col, b1), (gamma_col, gamma), (beta_col, beta)):
                for j in range(2):
                    act.dma_start(col[:, j:j + 1],
                                  vec[j * P:(j + 1) * P].rearrange("(p a) -> p a", a=1)).then_inc(weights_in, 16)
            act.dma_start(eps_col[:, :], eps.partition_broadcast(P)).then_inc(weights_in, 16)

            wide = read_flag(act, ENGINE.Activation)

            def load_weights():
                act.dma_start(w_base, weight.rearrange("b i o -> i b o")).then_inc(weights_in, 16)
                act.dma_start(w1_sb, w1[:, :]).then_inc(weights_in, 16)
                act.dma_start(w2_sb, w2.rearrange("(j p) o -> p j o", p=P)).then_inc(weights_in, 16)

            def zero_adjacency(s, j):
                size = HIGHS * SPREAD // GROUP
                nc.scalar.activation(adj_ring[:, s, j * size:(j + 1) * size], zero_col[:, 0:1].to_broadcast([P, size]),
                                     ACT.Copy).then_inc(adj_zeroed, 1)

            def count_step(i, s, zeroes, slots):
                g = i * RING + s
                zeroes = zeroes and s % PAIR == PAIR - 1
                slot = (s + 1) // PAIR % 2
                if zeroes and not (isinstance(i, int) and g < PAIR):
                    act.wait_ge(adj_out[slot], i * 16 + (16 if slot == 0 else 0))
                for j in range(GROUP):
                    act.wait_ge(tile_mm, (g + RING) * GROUP + j + 1)
                    act.wait_ge(adj_added, g * GROUP + j + 1)
                    nc.scalar.activation(count_stage[:, j % 2, :, :], adj_psum(j).rearrange("p (h n) -> p h n", n=WIN),
                                         ACT.Copy).then_inc(adj_copied, 1)
                    if zeroes:
                        zero_adjacency(slot, j)
                if slots:
                    copy_slots(g + RING, s)

            with act.If(wide < 1):
                act.sem_inc(adj_copied, 2)
                act.wait_ge(coef_ready, PIECES + 2)
                for j in range(GROUP):
                    zero_adjacency(0, j)
                for s in range(RING):
                    count_step(0, s, True, True)
                with act.Fori(1, GROUPS // RING - 1) as i:
                    for s in range(RING):
                        count_step(i, s, True, True)
                act.wait_ge(select_ready, GROUPS - RING)
                load_weights()
                for s in range(RING):
                    count_step(GROUPS // RING - 1, s, s < PAIR, False)

            def wide_slots(r):
                with act.If(wide > 0):
                    for s in range(RING):
                        act.wait_ge(gather_in[s], 16 * GROUP)
                    with act.Fori(0, T) as t:
                        act.wait_ge(wide_tile[r], t + 1)
                        nc.scalar.activation(src_slots[:, 0:1], src_t[:, bass.ds(t, 1)], ACT.Copy).then_inc(wide_slot[r], 1)

            wide_slots(0)
            with act.If(wide > 0):
                act.wait_ge(round_done[0], 1)
                load_weights()

            def relu_agg(k, s, n):
                act.wait_ge(agg_mm, k + 1)
                act.wait_ge(agg_turned, k + 1)
                nc.scalar.activation(layer_stage[:, s, 0:n], psum[:, s, 0:n], ACT.Relu,
                                     bias=bias0_col[:, 0:1]).then_inc(agg_relu, 1)

            def deviations(r):
                def stage(k, s, n):
                    c, rows = len(tiles_of(n)), min(n, P)
                    act.wait_ge(ln_var[r], k * CT + c)
                    nc.scalar.activation(ln_std[0:rows, s, 0:c], ln_mv[0:rows, s, 0:c, 1], ACT.Sqrt,
                                         bias=ln_eps_col[0:rows, 0:1]).then_inc(ln_std_ready[r], 1)
                return stage

            def keep_x1(k, s, n):
                act.wait_ge(x1_turned, k + 3)
                nc.scalar.activation(x1_t[:, span(k, n)], psum[:, 4 + s, 0:n], ACT.Copy).then_inc(x1_t_ready, 1)

            act.wait_ge(weights_in, 16 * 12)
            chunk_pipeline(act, relu_agg, deviations(0), lambda k, s, n: late(k) or keep_x1(k, s, n))
            for k in range(CHUNKS - 2, CHUNKS + 1):
                keep_x1(k, k % 2, REST if k == CHUNKS else CHUNK)

            wide_slots(1)

            def keep_hidden(k, s, n):
                act.wait_ge(hidden_mm, k + 1)
                for j in range(2):
                    nc.scalar.activation(hidden[:, j, span(k, n)], psum[:, 2 * s + j, 0:n], ACT.Identity,
                                         bias=b1_col[:, j:j + 1]).then_inc(hidden_ready, 1)

            chunk_pipeline(act, keep_hidden)
            act.wait_ge(bn_var, 2)
            nc.scalar.activation(bn_std[:, :], bn_mv[:, :, 1], ACT.Sqrt, bias=ln_eps_col[:, 0:1]).then_inc(bn_std_ready, 1)
            act.wait_ge(bn_ready, 1)

            def relu_hidden(k, s, n):
                act.wait_ge(out_mm, k + 1)
                for j in range(2):
                    nc.scalar.activation(relu_stage[:, s, j, 0:n], hidden[:, j, span(k, n)], ACT.Relu,
                                         bias=bn_shift[:, j:j + 1], scale=bn_scale[:, j:j + 1]).then_inc(relu_ready, 1)

            def normalise_out(k, s, n):
                act.wait_ge(shift_ready, k + 1)
                for i, rows in tiles_of(n):
                    nc.scalar.activation(out_stage[0:rows, bass.ds(k * CT + i, 1), :].rearrange("p t f -> p (t f)"),
                                         psum[0:rows, 2 + s, i * P:(i + 1) * P], ACT.Identity,
                                         bias=ln_shift[0:rows, s, i:i + 1],
                                         scale=ln_rstd[0:rows, s, i:i + 1]).then_inc(out_ready, 1)

            chunk_pipeline(act, relu_hidden, None, deviations(1), normalise_out, order=(0, 3, 2))

        @block.tensor
        def _(pe):
            pe.sem_inc(x1_turned, 2)
            pe.sem_inc(coef_mm, 4)
            pe.sem_inc(tile_mm, RING * GROUP)
            pe.sem_inc(nbr_mm, 2)
            pe.sem_inc(agg_turned, 2)
            pe.sem_inc(out_mm, 2)
            pe.sem_inc(out_turned, 2)

            def turn(rows, bank):
                for q in range(4):
                    last = nc.tensor.transpose(psum[:, bank, q * TQ:(q + 1) * TQ], rows[:, q, :], ident[0:TQ, 0:TQ])
                return last

            pe.wait_ge(const_ready, 2)
            pe.wait_ge(srcf_ready, 1)
            turn(srcf_rows, 0).then_inc(src_turned, 1)
            pe.wait_ge(cols_ready, 1)
            for bank, col in ((4, base_col), (5, span_col)):
                for q in range(4):
                    last = nc.tensor.matmul(psum[0:1, bank, q * TQ:(q + 1) * TQ], col[:, q:q + 1],
                                            ident[0:TQ, 0:TQ], start=True, stop=True)
            last.then_inc(cols_turned, 1)
            pe.wait_ge(rows_ready, 1)
            turn(rel_rows, 1)
            turn(dstf_rows, 2)
            turn(key_rows, 3).then_inc(turned, 1)

            def coefficient_products(m, s):
                pe.wait_ge(hot_built, m + 5)
                pe.wait_ge(coef_ready, m + 1)
                for j in range(PQ):
                    for part in range(3):
                        last = nc.tensor.matmul(psum[:, 6 + s % 2, j * 4 * B:(j + 1) * 4 * B],
                                                etype_hot[:, s, j * P:(j + 1) * P], comp_parts[:, part, :],
                                                start=(part == 0), stop=(part == 2))
                last.then_inc(coef_mm, 1)

            pe.wait_ge(norm_in, 16 * 3)
            turn(norm_rows, 0).then_inc(norm_turned, 1)
            pe.wait_ge(comp_split, 1)
            with pe.Fori(0, PIECES // 4) as i:
                for s in range(4):
                    coefficient_products(i * 4 + s, s)

            wide = read_flag(pe, ENGINE.PE)

            def narrow_sums():
                pe.wait_ge(coef_ready, PIECES + 2)
                def sums_start(i, s):
                    g = i * RING + s
                    turns, s = (i, s) if s < RING else (i + 1, 0)
                    pe.wait_ge(gather_in[s], turns * 16 * GROUP + 16 * GROUP)
                    pe.wait_ge(attrs_in[s % 2], turns * 64 + s // 2 * 32 + 32)
                    pe.wait_ge(select_ready, g + 1)
                    pe.wait_ge(added, g * GROUP + GROUP + 1)

                def sums_of_tile(s, j):
                    s = s % RING
                    ps = tile_psum(s % 2, j)
                    nc.tensor.matmul(ps[:, 0:B, :], gathered[:, s * GROUP + j, 0:F], weighted[:, s % 2, j, :, :],
                                     start=True, stop=True)
                    last = nc.tensor.matmul(ps[:, B, :], attrs[:, s % 2 * GROUP + j, :], hot[:, s % 2, j, :],
                                            start=True, stop=True)
                    if j == GROUP - 1:
                        last.then_inc(sums_mm, 1)

                def step(i, s, more):
                    g = i * RING + s
                    if more:
                        sums_start(i, s + 1)
                    for j in range(GROUP):
                        if more:
                            sums_of_tile(s + 1, j)
                        pe.wait_ge(key_ready, g * GROUP + j + 1)
                        pe.wait_ge(adj_copied, g * GROUP + j + 1)
                        nc.tensor.matmul(adj_psum(j), gathered[:, s * GROUP + j, F:ROW].bitcast(F16),
                                         key_hot[:, s % 2, j, :], start=True, stop=True).then_inc(tile_mm, 1)

                sums_start(0, 0)
                for j in range(GROUP):
                    sums_of_tile(0, j)
                with pe.Fori(0, GROUPS // RING - 1) as i:
                    for s in range(RING):
                        step(i, s, True)
                for s in range(RING):
                    step(GROUPS // RING - 1, s, s < RING - 1)

            def turn_late_x1():
                for k in range(CHUNKS - 2, CHUNKS + 1):
                    pe.wait_ge(parts_ready, k + 1)
                    pe.wait_ge(x1_t_ready, k + 1)
                    for i, rows in tiles_of(REST if k == CHUNKS else CHUNK):
                        for c in range(3):
                            last = nc.tensor.matmul(psum[:, 4 + k % 2, i * P:i * P + rows],
                                                    x1_parts[0:rows, k * CT + i, c, :], ident16[0:rows, 0:rows],
                                                    start=(c == 0), stop=(c == 2))
                    last.then_inc(x1_turned, 1)

            def neighbours():
                def block_sums(i, b, s, first=False):
                    pe.wait_ge(adj_in[s], i * 16 + 16)
                    pe.wait_ge(nbr_added, b * BLOCK + BLOCK + 1)
                    if first:
                        pe.wait_ge(agg_relu, CHUNKS + 3)
                        pe.wait_ge(parts_ready, CHUNKS - 2)
                    for h in range(HIGHS):
                        if first and h >= (CHUNKS - 2) * CT and h % CT == 0:
                            pe.wait_ge(parts_ready, h // CT + 1)
                        for c in range(3):
                            last = nc.tensor.matmul(psum[:, s, 0:BLOCK * SPREAD], x1_parts[:, h, c, :],
                                                    adj_blocks[s][:, :, h, :], start=(h + c == 0),
                                                    stop=(h == HIGHS - 1 and c == 2))
                    last.then_inc(nbr_mm, 1)

                block_sums(0, 0, 0, first=True)
                turn_late_x1()
                block_sums(0, 1, 1)
                with pe.Fori(1, BLOCKS // 2) as i:
                    for s in range(2):
                        block_sums(i, i * 2 + s, s)
                block_sums(BLOCKS // 2, BLOCKS - 1, 0)

            def edge_round(r):
                with pe.If(wide < 1):
                    if r == 0:
                        narrow_sums()
                    else:
                        neighbours()
                with pe.Else():
                    if r == 1:
                        turn_late_x1()
                    with pe.Fori(0, T) as t:
                        wait_alone(pe, wide_gather[r], t * 16 + 16)
                        if r == 0:
                            wait_alone(pe, wide_attr, t * 16 + 16)
                        with pe.Fori(0, WIDES) as w:
                            if r == 0:
                                pe.wait_ge(wide_select, t * WIDES + w + 1)
                                for h in range(B // 4):
                                    nc.tensor.matmul(psum[:, h, 0:4 * WIDE], gathered[:, 0, 0:F],
                                                     wide_weighted[:, 4 * h:4 * h + 4, :], start=True, stop=True)
                                last = nc.tensor.matmul(wide_psum(B), attrs[:, 0, :], wide_hot_sb[:, :],
                                                        start=True, stop=True)
                            else:
                                pe.wait_ge(wide_hot[r], t * WIDES + w + 1)
                                last = nc.tensor.matmul(wide_psum(B), gathered[:, 0, 0:F], wide_hot_sb[:, :],
                                                        start=True, stop=True)
                            last.then_inc(wide_mm[r], 1)

            edge_round(0)
            pe.wait_ge(round_done[0], 1)

            def turn_chunk(bank, source, n):
                for i, rows in tiles_of(n):
                    last = nc.tensor.transpose(psum[0:rows, bank, i * P:(i + 1) * P],
                                               source[:, i * P:i * P + rows], ident[:, :])
                return last

            def through_bases(k, s, n):
                pe.wait_ge(agg_relu, k + 1)
                for b in range(B):
                    last = nc.tensor.matmul(psum[:, s, 0:n], w_base[:, b, :], sums[:, b, span(k, n)],
                                            start=(b == 0), stop=(b == B - 1))
                last.then_inc(agg_mm, 1)

            def turn_agg(k, s, n):
                pe.wait_ge(agg_relu, k + 3)
                pe.wait_ge(res_ready[0], k + 1)
                turn_chunk(2 + s, layer_stage[:, s, :], n).then_inc(agg_turned, 1)

            def turn_x1(k, s, n):
                if late(k):
                    return
                pe.wait_ge(x1_ready, (k + 3) * CT)
                pe.wait_ge(x1_t_ready, k + 1)
                for i in range(CT):
                    last = nc.tensor.transpose(psum[:, 4 + s, i * P:(i + 1) * P], node_stage[:, s, i, :], ident[:, :])
                last.then_inc(x1_turned, 1)

            pe.wait_ge(weights_in, 16 * 12)
            chunk_pipeline(pe, through_bases, turn_agg, turn_x1)
            edge_round(1)

            def into_hidden(k, s, n):
                pe.wait_ge(hidden_ready, k * 2 + 2)
                for j in range(2):
                    last = nc.tensor.matmul(psum[:, 2 * s + j, 0:n], w1_sb[:, j * P:(j + 1) * P],
                                            sums[:, B, span(k, n)], start=True, stop=True)
                last.then_inc(hidden_mm, 1)

            pe.wait_ge(round_done[1], 1)
            chunk_pipeline(pe, into_hidden)
            pe.wait_ge(bn_ready, 1)

            def into_out(k, s, n):
                pe.wait_ge(relu_ready, k * 2 + 2)
                pe.wait_ge(out_t_ready, k + 1)
                for j in range(2):
                    last = nc.tensor.matmul(psum[:, s, 0:n], w2_sb[:, j, :], relu_stage[:, s, j, 0:n],
                                            start=(j == 0), stop=(j == 1))
                last.then_inc(out_mm, 1)

            def turn_out(k, s, n):
                pe.wait_ge(out_t_ready, k + 3)
                pe.wait_ge(out_ready, k * CT + CT)
                turn_chunk(2 + s, layer_stage[:, s, :], n).then_inc(out_turned, 1)

            chunk_pipeline(pe, into_out, turn_out)

        @block.vector
        def _(dve):
            steps = [0]

            def link(instruction):
                steps[0] += 1
                instruction.then_inc(prep, 1)
                dve.wait_ge(prep, steps[0])

            dve.sem_inc(hot_built, 4)
            dve.sem_inc(coef_ready, 2)
            dve.sem_inc(added, 2 * GROUP + 1)
            dve.sem_inc(adj_added, 2)
            dve.sem_inc(nbr_added, 2 * BLOCK + 1)
            dve.sem_inc(wide_add[0], 1)
            dve.sem_inc(wide_add[1], 1)
            dve.sem_inc(wide_tile[0], 1)
            dve.sem_inc(wide_tile[1], 1)
            dve.sem_inc(x1_ready, 2 * CT)
            dve.sem_inc(res_ready[0], 2)
            dve.sem_inc(out_t_ready, 2)

            dve.wait_ge(src_in, 16 * 3)
            nc.vector.tensor_copy(srcf_rows[:, :, :], src_rows[:, :, :]).then_inc(srcf_ready, 1)
            comp, comp_rest = (c[:, :, :].rearrange("p q b -> p (q b)") for c in (comp_diag, comp_left))
            dve.wait_ge(comp_in, 64)
            link(nc.vector.tensor_scalar(comp_parts[:, 0, :], comp, 1.0, None, ALU.mult))
            link(nc.vector.tensor_tensor(comp_rest, comp, comp_parts[:, 0, :], ALU.subtract))
            link(nc.vector.tensor_scalar(comp_parts[:, 1, :], comp_rest, 1.0, None, ALU.mult))
            nc.vector.tensor_tensor(comp_parts[:, 2, :], comp_rest, comp_parts[:, 1, :], ALU.subtract).then_inc(comp_split, 1)
            dve.wait_ge(src_turned, 1)
            nc.vector.tensor_copy(src_t[:, :], psum[:, 0, 0:T]).then_inc(src_t_ready, 1)
            dve.wait_ge(etype_rows_in, 16 * 3)
            nc.vector.tensor_copy(etype16_rows[:, :, :], etype_rows[:, :, :]).then_inc(etype16_ready, 1)
            dve.wait_ge(rows_in, 16 * 3)
            link(nc.vector.tensor_copy(dstf_rows[:, :, :], dst_rows[:, :, :]))
            nc.vector.tensor_reduce(base_col[:, :], dstf_rows[:, :, :], AX_X, ALU.min)
            link(nc.vector.tensor_reduce(high_col[:, :], dstf_rows[:, :, :], AX_X, ALU.max))
            nc.vector.tensor_tensor(span_col[:, :], high_col[:, :], base_col[:, :], ALU.subtract).then_inc(cols_ready, 1)
            nc.vector.tensor_scalar(high_rows, src_rows, P.bit_length() - 1, None, ALU.logical_shift_right)
            link(nc.vector.tensor_tensor(rel_rows, dstf_rows[:, :, :],
                                         base_col[:, :].unsqueeze(2).to_broadcast([TQ, 4, P]), ALU.subtract))
            nc.vector.scalar_tensor_tensor(key_rows, high_rows, float(WIN), rel_rows, ALU.mult,
                                           ALU.add).then_inc(rows_ready, 1)
            coef_view = coef[:, :, :].rearrange("p (q t) b -> p t q b", q=4)
            norm_view = norm_t[:, :].rearrange("p (q t) -> p t q", q=4)

            def relation_hot(i, m, s):
                dve.wait_ge(etype_in[s], i * 64 + 64)
                dve.wait_ge(coef_mm, m + 1)
                nc.vector.tensor_scalar(etype_hot[:, s, :], etype_bc[:, s, :], relation_col[:, 0:1], None,
                                        ALU.is_equal).then_inc(hot_built, 1)

            def coefficients(m, s):
                dve.wait_ge(coef_mm, m + 5)
                nc.vector.tensor_tensor(
                    coef_view[:, bass.ds(m * PQ, PQ), :, :],
                    psum[:, 6 + s % 2, 0:PQ * 4 * B].rearrange("p (t q b) -> p t q b", q=4, b=B),
                    norm_view[:, bass.ds(m * PQ, PQ), :].unsqueeze(3).to_broadcast([P, PQ, 4, B]),
                    ALU.mult).then_inc(coef_ready, 1)

            def places_hot(g, s):
                nc.vector.tensor_tensor(
                    hot[:, s % 2, :, :], rel_t[:, bass.ds(g * GROUP, GROUP)].unsqueeze(2).to_broadcast([P, GROUP, WIN]),
                    iota_win[:, :].unsqueeze(1).to_broadcast([P, GROUP, WIN]), ALU.is_equal).then_inc(hot_ready, 1)

            def weight_hot(g, s):
                dve.wait_ge(hot_ready, g + 1)
                nc.vector.tensor_tensor(
                    weighted[:, s % 2, :, :, :], hot[:, s % 2, :, :].unsqueeze(2).to_broadcast([P, GROUP, B, WIN]),
                    coef[:, bass.ds(g * GROUP, GROUP), :].unsqueeze(3).to_broadcast([P, GROUP, B, WIN]),
                    ALU.mult).then_inc(select_ready, 1)

            dve.wait_ge(const_ready, 10)
            for s in range(2):
                relation_hot(0, s, s)
            dve.wait_ge(relations_out, 16)
            dve.wait_ge(norm_turned, 1)
            nc.vector.tensor_copy(norm_t[:, :], psum[:, 0, 0:T])
            dve.wait_ge(cols_turned, 1)
            base_psum = psum[0:1, 4, 0:T].rearrange("p (g j) -> p g j", j=GROUP)
            behind = base_row[:, :, GROUP:2 * GROUP]
            link(nc.vector.tensor_copy(base_row[:, :, 0:GROUP], base_psum))
            nc.vector.tensor_reduce(flags[:, 0:1], psum[0:1, 5, 0:T], AX_X, ALU.max)
            by_pair = lambda ap: ap.rearrange("p (g h) j -> p g h j", h=PAIR)
            link(nc.vector.tensor_tensor(by_pair(behind), by_pair(base_psum),
                                         by_pair(base_row[:, :, :])[:, :, 0:1, 0:1].to_broadcast([1, PAIRS, PAIR, GROUP]),
                                         ALU.subtract))
            nc.vector.tensor_reduce(flags[:, 1:2], behind.rearrange("p g j -> p g j"), AX_XY, ALU.max)
            link(nc.vector.tensor_reduce(flags[:, 2:3], behind, AX_XY, ALU.min))
            nc.vector.tensor_scalar(flags[:, 4:5], flags[:, 0:1], float(WIN), None, ALU.is_ge)
            nc.vector.tensor_scalar(flags[:, 5:6], flags[:, 1:2], float(SPREAD - WIN + 1), None, ALU.is_ge)
            link(nc.vector.tensor_scalar(flags[:, 6:7], flags[:, 2:3], 0.0, None, ALU.is_lt))
            dve.wait_ge(turned, 1)
            nc.vector.tensor_reduce(wide_flag[:, :], flags[:, 4:7], AX_X, ALU.max).then_inc(flag_ready, 1)

            def columns():
                nc.vector.tensor_copy(rel_t[:, :], psum[:, 1, 0:T])
                nc.vector.tensor_copy(key_t[:, :], psum[:, 3, 0:T])
                nc.vector.tensor_copy(dst_t[:, :], psum[:, 2, 0:T])
                dve.wait_ge(const_ready, 13)
                link(nc.vector.tensor_scalar(own_col[:, :], iota_col[:, :], float(P - FRESH), None, ALU.is_ge))
                last_cols = [cols[:, T - 1:T] for cols in (rel_t, key_t, dst_t)]
                for last_col in last_cols:
                    last = nc.vector.tensor_scalar(last_col, last_col, FAR, own_col[:, 0:1], ALU.add, ALU.mult)
                link(last)
                for last_col in last_cols:
                    last = nc.vector.tensor_scalar(last_col, last_col, -FAR, None, ALU.add)
                link(last)

            for s in range(2, 4):
                relation_hot(0, s, s)
            for s in range(4):
                coefficients(s, s)
                relation_hot(1, 4 + s, s)
                if s == 0:
                    columns()
                if s == 1:
                    dve.wait_ge(coef_ready, 4)
                    for g in range(2):
                        places_hot(g, g)
                        weight_hot(g, g)
            for s in range(4):
                coefficients(4 + s, s)
            dve.wait_ge(coef_ready, PIECES + 2)
            dve.wait_ge(zeroed, 1)

            wide = read_flag(dve, ENGINE.DVE)

            def keys_hot(g, s, j):
                nc.vector.tensor_scalar(key_hot[:, s % 2, j, :], iota_key[:, :], key_t[:, bass.ds(g * GROUP + j, 1)],
                                        None, ALU.is_equal).then_inc(key_ready, 1)

            def step(i, s, select_more, keys_more):
                g = i * RING + s

                def places(lo, most, why):
                    return nc.values_load_multi_w_load_instructions(
                        base_row[0:1, bass.ds(g, 1), lo:lo + GROUP].rearrange("p g j -> p (g j)"),
                        engines=(ENGINE.DVE,), min_val=0, max_val=most, skip_runtime_bounds_check_because=why)[1]

                bases = places(0, N - 1, "bases are node numbers")
                offsets = places(GROUP, SPREAD - WIN, "the flag says so")
                dve.wait_ge(sums_mm, g + 1)
                if select_more:
                    places_hot(g + 2, s)
                for j in range(GROUP):
                    window = sums[:, :, bass.ds(bases[j], WIN)]
                    counts = adj_ring[:, s // PAIR, :].rearrange("p (h n) -> p h n", n=SPREAD)[:, :, bass.ds(offsets[j], WIN)]
                    dve.wait_ge(added, (g + 2) * GROUP + j + 1)
                    nc.vector.tensor_tensor(window, tile_psum(s % 2, j), window, ALU.add).then_inc(added, 1)
                    if keys_more:
                        keys_hot(g + 1, s + 1, j)
                    if j == 0:
                        dve.wait_ge(adj_zeroed, (i * BLOCK + s // PAIR + 1) * GROUP)
                    dve.wait_ge(adj_copied, g * GROUP + j + 3)
                    dve.wait_ge(adj_added, g * GROUP + j + 2)
                    nc.vector.tensor_tensor(counts, count_stage[:, j % 2, :, :], counts, ALU.add).then_inc(adj_added, 1)
                    if select_more and j == 0:
                        weight_hot(g + 2, s)

            def narrow_sums():
                for j in range(GROUP):
                    keys_hot(0, 0, j)
                with dve.Fori(0, GROUPS // RING - 1) as i:
                    for s in range(RING):
                        step(i, s, True, True)
                for s in range(RING):
                    step(GROUPS // RING - 1, s, s < RING - 2, s < RING - 1)
                dve.wait_ge(added, T + 2 * GROUP + 1)

            def neighbours():
                def block(b, s):
                    firsts = nc.values_load_multi_w_load_instructions(
                        base_row[0:1, :, :].rearrange("p (g h) j -> p g (h j)", h=PAIR)[:, bass.ds(b * BLOCK, BLOCK), 0],
                        engines=(ENGINE.DVE,), min_val=0,
                        max_val=N - 1, skip_runtime_bounds_check_because="bases are node numbers")[1]
                    dve.wait_ge(nbr_mm, b + 3)
                    for j in range(BLOCK):
                        window = sums_flat[:, bass.ds(firsts[j] + B * NP, SPREAD)]
                        dve.wait_ge(nbr_added, b * BLOCK + 2 * BLOCK + 1 + j)
                        nc.vector.tensor_tensor(window, psum[:, s, j * SPREAD:(j + 1) * SPREAD], window,
                                                ALU.add).then_inc(nbr_added, 1)

                with dve.Fori(0, BLOCKS // 2) as i:
                    for s in range(2):
                        block(i * 2 + s, s)
                block(BLOCKS - 1, 0)
                dve.wait_ge(nbr_added, PAIRS + 2 * BLOCK + 1)

            def edge_round(r):
                with dve.If(wide < 1):
                    if r == 0:
                        narrow_sums()
                    else:
                        neighbours()
                with dve.Else():
                    adds = 2 if r == 0 else 1
                    with dve.Fori(0, T) as t:
                        with dve.Fori(0, WIDES) as w:
                            j = t * WIDES + w
                            dve.wait_ge(wide_add[r], j * adds + 1)
                            nc.vector.tensor_scalar(wide_hot_sb[:, :], iota_wide[:, :], wide_starts[:, bass.ds(w, 1)],
                                                    dst_t[:, bass.ds(t, 1)], ALU.add, ALU.is_equal).then_inc(wide_hot[r], 1)
                            if r == 0:
                                dve.wait_ge(wide_hot[r], j + 1)
                                nc.vector.tensor_tensor(
                                    wide_weighted[:, :, :], wide_hot_sb[:, :].unsqueeze(1).to_broadcast([P, B, WIDE]),
                                    coef[:, bass.ds(t, 1), :].rearrange("p t b -> p (t b)").unsqueeze(2)
                                    .to_broadcast([P, B, WIDE]), ALU.mult).then_inc(wide_select, 1)
                            dve.wait_ge(wide_mm[r], j + 1)
                            if r == 0:
                                window = sums[:, 0:B, bass.ds(w * WIDE, WIDE)].rearrange("p (h b) n -> p h b n", b=4)
                                nc.vector.tensor_tensor(
                                    window, psum[:, 0:B // 4, 0:4 * WIDE].rearrange("p h (b n) -> p h b n", b=4),
                                    window, ALU.add).then_inc(wide_add[r], 1)
                            window = sums[:, B, bass.ds(w * WIDE, WIDE)]
                            nc.vector.tensor_tensor(window, wide_psum(B), window, ALU.add).then_inc(wide_add[r], 1)
                        dve.sem_inc(wide_tile[r], 1)
                    dve.wait_ge(wide_add[r], T * WIDES * adds + 1)
                dve.sem_inc(round_done[r], 1)

            edge_round(0)

            def statistics(r, k, s, n, source):
                for i, rows in tiles_of(n):
                    nc.vector.bn_stats(ln_part[0:rows, s, i, :], source(i, rows)).then_inc(ln_stats[r], 1)
                wait_alone(dve, ln_stats[r], k * CT + len(tiles_of(n)))
                for i, rows in tiles_of(n):
                    nc.vector.bn_aggr(ln_mv[0:rows, s, i, :], ln_part[0:rows, s, i, :]).then_inc(ln_var[r], 1)

            def normalise(r, k, s, n, source, target, signal):
                c, top = len(tiles_of(n)), min(n, P)
                dve.wait_ge(ln_std_ready[r], k + 1)
                nc.vector.reciprocal(ln_rstd[0:top, s, 0:c], ln_std[0:top, s, 0:c]).then_inc(ln_rstd_ready[r], 1)
                dve.wait_ge(ln_rstd_ready[r], k + 1)
                for i, rows in tiles_of(n):
                    nc.vector.tensor_scalar(target(i, rows), source(i, rows), ln_mv[0:rows, s, i, 0:1],
                                            ln_rstd[0:rows, s, i:i + 1], ALU.subtract, ALU.mult).then_inc(signal, 1)

            def first_residual(k, s, n):
                dve.wait_ge(x_in[s], (k - s) * 8 + 16)
                dve.wait_ge(agg_turned, k + 3)
                dve.wait_ge(x1_out[s], (k - s) * 8 + 16)
                if not (isinstance(k, int) and k == CHUNKS):
                    dve.wait_ge(x1_turned, k + 1)
                c, rows = len(tiles_of(n)), min(n, P)
                nc.vector.tensor_tensor(node_stage[0:rows, s, 0:c, :],
                                        psum[0:rows, 2 + s, 0:c * P].rearrange("p (t f) -> p t f", f=F),
                                        x_stage[0:rows, s, 0:c, :], ALU.add).then_inc(res_ready[0], 1)
                dve.wait_ge(res_ready[0], k + 3)
                statistics(0, k, s, n, lambda i, rows: node_stage[0:rows, s, i, :])

            def first_norm(k, s, n):
                tile = lambda i, rows: node_stage[0:rows, s, i, :]
                normalise(0, k, s, n, tile, tile, x1_ready)

            def split(k, s, n):
                c, rows = len(tiles_of(n)), min(n, P)
                x1, rest = node_stage[0:rows, s, 0:c, :], left[0:rows, s, 0:c, :]
                part = [x1_parts[0:rows, bass.ds(k * CT, c), i, :] for i in range(3)]
                dve.wait_ge(x1_ready, (k + 2) * CT + c)
                nc.vector.tensor_scalar(part[0], x1, 1.0, None, ALU.mult).then_inc(parts_step, 1)
                dve.wait_ge(parts_step, k * 3 + 1)
                nc.vector.tensor_tensor(rest, x1, part[0], ALU.subtract).then_inc(parts_step, 1)
                dve.wait_ge(parts_step, k * 3 + 2)
                nc.vector.tensor_scalar(part[1], rest, 1.0, None, ALU.mult).then_inc(parts_step, 1)
                dve.wait_ge(parts_step, k * 3 + 3)
                nc.vector.tensor_tensor(part[2], rest, part[1], ALU.subtract).then_inc(parts_ready, 1)

            link(nc.vector.memset(x1_parts[:, HIGHS - 1, :, :], 0.0))

            def norm_and_split(k, s, n):
                first_norm(k, s, n)
                split(k, s, n)

            chunk_pipeline(dve, first_residual, norm_and_split, order=(1, 0))

            link(nc.vector.tensor_scalar(one_eps[:, :], eps_col[:, :], 1.0, None, ALU.add))

            def add_own(k, s, n):
                dve.wait_ge(x1_t_ready, k + 3)
                total = sums[:, B, span(k, n)]
                nc.vector.scalar_tensor_tensor(total, x1_t[:, span(k, n)], one_eps[:, 0:1], total,
                                               ALU.mult, ALU.add).then_inc(own_added, 1)

            chunk_pipeline(dve, add_own)
            dve.wait_ge(own_added, CHUNKS + 1)
            edge_round(1)

            def hidden_stats(k, s, n):
                dve.wait_ge(hidden_ready, k * 2 + 6)
                for j in range(2):
                    nc.vector.bn_stats(bn_part[:, j, bass.ds(k, 1), :].rearrange("p a c -> p (a c)"),
                                       hidden[:, j, span(k, n)]).then_inc(bn_step, 1)

            chunk_pipeline(dve, hidden_stats)
            dve.wait_ge(bn_step, 2 * (CHUNKS + 1))
            for j in range(2):
                nc.vector.bn_aggr(bn_mv[:, j, :], bn_part[:, j, :, :].rearrange("p k c -> p (k c)")).then_inc(bn_var, 1)
            dve.wait_ge(bn_std_ready, 1)
            link(nc.vector.reciprocal(bn_rstd[:, :], bn_std[:, :]))
            link(nc.vector.tensor_tensor(bn_scale[:, :], bn_rstd[:, :], gamma_col[:, :], ALU.mult))
            link(nc.vector.tensor_tensor(bn_ms[:, :], bn_mv[:, :, 0], bn_scale[:, :], ALU.mult))
            nc.vector.tensor_tensor(bn_shift[:, :], beta_col[:, :], bn_ms[:, :], ALU.subtract).then_inc(bn_ready, 1)

            def second_residual(k, s, n):
                dve.wait_ge(out_mm, k + 3)
                dve.wait_ge(out_turned, k + 1)
                nc.vector.scalar_tensor_tensor(layer_stage[:, s, 0:n], psum[:, s, 0:n], b2_col[:, 0:1],
                                               x1_t[:, span(k, n)], ALU.add, ALU.add).then_inc(out_t_ready, 1)

            def out_tile(s, i, rows):
                return psum[0:rows, 2 + s, i * P:(i + 1) * P]

            def second_stats(k, s, n):
                dve.wait_ge(out_turned, k + 3)
                statistics(1, k, s, n, lambda i, rows: out_tile(s, i, rows))

            def second_shift(k, s, n):
                c, top = len(tiles_of(n)), min(n, P)
                dve.wait_ge(ln_std_ready[1], k + 1)
                dve.wait_ge(out_ready, k * CT + CT)
                nc.vector.reciprocal(ln_rstd[0:top, s, 0:c], ln_std[0:top, s, 0:c]).then_inc(ln_rstd_ready[1], 1)
                dve.wait_ge(ln_rstd_ready[1], k + 1)
                nc.vector.scalar_tensor_tensor(ln_shift[0:top, s, 0:c], ln_mv[0:top, s, 0:c, 0], -1.0,
                                               ln_rstd[0:top, s, 0:c], ALU.mult, ALU.mult).then_inc(shift_ready, 1)

            chunk_pipeline(dve, second_residual, second_stats, second_shift, order=(2, 1, 0))


_INS = ['x', 'src', 'dst', 'edge_attr_128', 'edge_type_32', 'edge_weight1', 'L0_gnn_weight', 'L0_gnn_w_comp',
        'L0_gnn_bias_param', 'L1_gnn_eps', 'L1_gnn_W1', 'L1_gnn_b1', 'L1_gnn_gamma', 'L1_gnn_beta', 'L1_gnn_W2',
        'L1_gnn_b2']


def kernel(**inputs):
    import numpy as _np
    import concourse.bacc as _bacc
    from concourse import mybir as _mybir
    from concourse.bass_utils import run_bass_kernel_spmd as _run

    nc = _bacc.Bacc("TRN2", target_bir_lowering=False, num_devices=1)
    arrays, args = {}, []
    for name in _INS:
        a = _np.ascontiguousarray(inputs[name])
        if name == 'edge_weight1':
            a = a.reshape(-1)
        arrays[f"in_{name}_dram"] = a
        args.append(nc.dram_tensor(f"in_{name}_dram", a.shape, _mybir.dt.from_np(a.dtype), kind="ExternalInput").ap())
    args.append(nc.dram_tensor("out_0_dram", inputs['x'].shape, _mybir.dt.float32, kind="ExternalOutput").ap())
    gnn_resnorm_kernel(nc, *args)
    r = _run(nc, [arrays], core_ids=[0])
    return r.results[0]["out_0_dram"]
```
